# Optimizing a Trainium2 kernel written in Bass

```python
import numpy as np
import jax
import jax.numpy as jnp

def _softmax(x, axis=-1):
    return jax.nn.softmax(x, axis=axis)

def _gelu(x):
    return jax.nn.gelu(x, approximate=True)

def _silu(x):
    return jax.nn.silu(x)

def _sigmoid(x):
    return jax.nn.sigmoid(x)

def _layernorm(x, axis=-1, eps=1e-05):
    m = jnp.mean(x, axis=axis, keepdims=True)
    v = jnp.var(x, axis=axis, keepdims=True)
    return (x - m) / jnp.sqrt(v + eps)

def _scatter_add(tgt, idx, src, axis=0):
    return tgt.at[idx].add(src)

def _segment_sum(src, seg, n):
    return jax.ops.segment_sum(src, seg, n)
kernel_name = 'mk_metaformer_d1_conv_nhwc256_r4_55d271'

def setup_inputs(seed: int=0):
    np.random.seed(seed)
    _w = jnp.asarray

    def _rec_inputs():
        import jax
        import jax.numpy as jnp
        _gk = jax.random.key(seed)
        x = 7.22e-05 + 1 * jax.random.normal(jax.random.fold_in(_gk, 1), (1, 16, 128, 64), jnp.float32)
        return x
    x = _rec_inputs()

    def _L0_conv_setup():
        import jax, jax.numpy as jnp
        import numpy as np
        N_DIMS = 64
        N_HEADS = 8
        DIM_HEAD = 16
        INNER = N_HEADS * DIM_HEAD
        EPS = 1e-05

        def _layernorm(x, g, b):
            mean = x.mean(-1, keepdims=True)
            var = ((x - mean) ** 2).mean(-1, keepdims=True)
            return g * (x - mean) / jnp.sqrt(var + EPS) + b
        key = jax.random.key(seed)
        ks = jax.random.split(key, 8)
        b, h, w, d = (1, 16, 128, N_DIMS)
        x = jax.random.normal(ks[0], (b, h, w, d), dtype=jnp.float32)
        s_in = 1.0 / np.sqrt(d)
        s_inner = 1.0 / np.sqrt(INNER)
        return {'x': x, 'ln_g': jnp.ones((d,), jnp.float32), 'ln_b': jnp.zeros((d,), jnp.float32), 'Wq': jax.random.normal(ks[1], (d, INNER), jnp.float32) * s_in, 'Wkv': jax.random.normal(ks[2], (d, 2 * INNER), jnp.float32) * s_in, 'Wg': jax.random.normal(ks[3], (d, INNER), jnp.float32) * 0.02, 'bg': jnp.ones((INNER,), jnp.float32), 'Wo': jax.random.normal(ks[4], (INNER, d), jnp.float32) * s_inner, 'bo': jnp.zeros((d,), jnp.float32)}
    _L0_conv_all = _L0_conv_setup()
    _L0_conv_in = {k: v for k, v in _L0_conv_all.items() if k in ('ln_g', 'ln_b', 'Wq', 'Wkv', 'Wg', 'bg', 'Wo', 'bo')}
    del _L0_conv_all

    def _L0_ffn_setup():
        import math
        import jax, jax.numpy as jnp
        import numpy as np
        CAPACITY_FACTOR = 1.25
        TOP_K = 2
        LN_EPS = 1e-05

        def _layer_norm(x, gamma, beta):
            mu = jnp.mean(x, axis=-1, keepdims=True)
            var = jnp.var(x, axis=-1, keepdims=True)
            return (x - mu) * jax.lax.rsqrt(var + LN_EPS) * gamma + beta
        key = jax.random.key(seed)
        ks = jax.random.split(key, 4)
        B, S, D, F, E = (8, 1024, 64, 128, 8)
        x = jax.random.normal(ks[0], (B, S, D), dtype=jnp.float32)
        Wr = jax.random.normal(ks[1], (D, E), dtype=jnp.float32) / np.sqrt(D)
        br = jnp.zeros((E,), jnp.float32)
        W1 = jax.random.normal(ks[2], (E, D, F), dtype=jnp.float32) / np.sqrt(D)
        b1 = jnp.zeros((E, F), jnp.float32)
        W2 = jax.random.normal(ks[3], (E, F, D), dtype=jnp.float32) / np.sqrt(F)
        b2 = jnp.zeros((E, D), jnp.float32)
        gamma = jnp.ones((D,), jnp.float32)
        beta = jnp.zeros((D,), jnp.float32)
        return {'x': x, 'Wr': Wr, 'br': br, 'W1': W1, 'b1': b1, 'W2': W2, 'b2': b2, 'gamma': gamma, 'beta': beta}
    _L0_ffn_all = _L0_ffn_setup()
    _L0_ffn_in = {k: v for k, v in _L0_ffn_all.items() if k in ('Wr', 'br', 'W1', 'b1', 'W2', 'b2', 'gamma', 'beta')}
    del _L0_ffn_all
    return {'x': x, 'L0_conv_ln_g': _L0_conv_in['ln_g'], 'L0_conv_ln_b': _L0_conv_in['ln_b'], 'L0_conv_Wq': _L0_conv_in['Wq'], 'L0_conv_Wkv': _L0_conv_in['Wkv'], 'L0_conv_Wg': _L0_conv_in['Wg'], 'L0_conv_bg': _L0_conv_in['bg'], 'L0_conv_Wo': _L0_conv_in['Wo'], 'L0_conv_bo': _L0_conv_in['bo'], 'L0_ffn_Wr': _L0_ffn_in['Wr'], 'L0_ffn_br': _L0_ffn_in['br'], 'L0_ffn_W1': _L0_ffn_in['W1'], 'L0_ffn_b1': _L0_ffn_in['b1'], 'L0_ffn_W2': _L0_ffn_in['W2'], 'L0_ffn_b2': _L0_ffn_in['b2'], 'L0_ffn_gamma': _L0_ffn_in['gamma'], 'L0_ffn_beta': _L0_ffn_in['beta']}

def reference(x, L0_conv_ln_g, L0_conv_ln_b, L0_conv_Wq, L0_conv_Wkv, L0_conv_Wg, L0_conv_bg, L0_conv_Wo, L0_conv_bo, L0_ffn_Wr, L0_ffn_br, L0_ffn_W1, L0_ffn_b1, L0_ffn_W2, L0_ffn_b2, L0_ffn_gamma, L0_ffn_beta):
    import jax
    import jax.numpy as jnp

    def _L0_conv_ref(x, ln_g, ln_b, Wq, Wkv, Wg, bg, Wo, bo):
        import jax, jax.numpy as jnp
        import numpy as np
        N_DIMS = 64
        N_HEADS = 8
        DIM_HEAD = 16
        INNER = N_HEADS * DIM_HEAD
        EPS = 1e-05

        def _layernorm(x, g, b):
            mean = x.mean(-1, keepdims=True)
            var = ((x - mean) ** 2).mean(-1, keepdims=True)
            return g * (x - mean) / jnp.sqrt(var + EPS) + b
        b, h, w, d = x.shape
        xn = _layernorm(x, ln_g, ln_b)
        xf = xn.reshape(b * h, w, d)
        q = xf @ Wq
        kv = xf @ Wkv
        k, v = (kv[..., :INNER], kv[..., INNER:])

        def split_heads(t):
            B, n, _ = t.shape
            return t.reshape(B, n, N_HEADS, DIM_HEAD).transpose(0, 2, 1, 3)
        q, k, v = map(split_heads, (q, k, v))
        q = q * DIM_HEAD ** (-0.5)
        dots = jnp.einsum('bhid,bhjd->bhij', q, k)
        dots = dots - jax.lax.stop_gradient(dots.max(axis=-1, keepdims=True))
        attn = jax.nn.softmax(dots, axis=-1)
        out = jnp.einsum('bhij,bhjd->bhid', attn, v)
        out = out.transpose(0, 2, 1, 3).reshape(b * h, w, INNER)
        gates = xf @ Wg + bg
        out = out * jax.nn.sigmoid(gates)
        out = out @ Wo + bo
        return out.reshape(b, h, w, d)

    def _L0_ffn_ref(x, Wr, br, W1, b1, W2, b2, gamma, beta):
        import math
        import jax, jax.numpy as jnp
        import numpy as np
        CAPACITY_FACTOR = 1.25
        TOP_K = 2
        LN_EPS = 1e-05

        def _layer_norm(x, gamma, beta):
            mu = jnp.mean(x, axis=-1, keepdims=True)
            var = jnp.var(x, axis=-1, keepdims=True)
            return (x - mu) * jax.lax.rsqrt(var + LN_EPS) * gamma + beta
        B, S, D = x.shape
        E = Wr.shape[1]
        N = B * S
        K = TOP_K
        logits = jnp.mean(x, axis=1) @ Wr + br
        routing_weights = jax.nn.softmax(logits, axis=-1)
        capacity = float(math.ceil(N * CAPACITY_FACTOR / E))
        expected_loads = routing_weights.sum(axis=0) * (N / B)
        scale = jnp.where(expected_loads > capacity, capacity / expected_loads, 1.0)
        routing_weights = jax.nn.softmax(routing_weights * scale, axis=-1)
        rw_tok = jnp.broadcast_to(routing_weights[:, None, :], (B, S, E)).reshape(N, E)
        top_w, top_i = jax.lax.top_k(rw_tok, K)
        top_w = jax.nn.softmax(top_w, axis=-1)
        xf = x.reshape(N, D)
        h = jax.nn.gelu(jnp.einsum('nd,edf->enf', xf, W1) + b1[:, None, :], approximate=False)
        y = jnp.einsum('enf,efd->end', h, W2) + b2[:, None, :]
        w_dense = jnp.zeros((N, E), x.dtype).at[jnp.arange(N)[:, None], top_i].add(top_w)
        out = jnp.einsum('ne,end->nd', w_dense, y).reshape(B, S, D)
        out = _layer_norm(out + x, gamma, beta)
        return out

    def _gn(v, G=32, eps=1e-05):
        B_, H_, W_, C_ = v.shape
        g = v.reshape(B_, H_, W_, G, C_ // G)
        m = jnp.mean(g, axis=(1, 2, 4), keepdims=True)
        s = jnp.var(g, axis=(1, 2, 4), keepdims=True)
        return ((g - m) / jnp.sqrt(s + eps)).reshape(v.shape)

    def _ln_c(v, eps=1e-06):
        m = jnp.mean(v, axis=-1, keepdims=True)
        s = jnp.var(v, axis=-1, keepdims=True)
        return (v - m) / jnp.sqrt(s + eps)

    def _ln_t(v, eps=1e-05):
        m = jnp.mean(v, axis=-1, keepdims=True)
        s = jnp.var(v, axis=-1, keepdims=True)
        return (v - m) / jnp.sqrt(s + eps)

    def _to_tokens(v):
        B_, H_, W_, C_ = v.shape
        return v.reshape(B_, H_ * W_, C_)

    def _from_tokens(t, like):
        return t.reshape(like.shape)
    x = x + _L0_conv_ref(_ln_c(x), L0_conv_ln_g, L0_conv_ln_b, L0_conv_Wq, L0_conv_Wkv, L0_conv_Wg, L0_conv_bg, L0_conv_Wo, L0_conv_bo)
    t = _to_tokens(x)
    t = t + _L0_ffn_ref(_ln_t(t), L0_ffn_Wr, L0_ffn_br, L0_ffn_W1, L0_ffn_b1, L0_ffn_W2, L0_ffn_b2, L0_ffn_gamma, L0_ffn_beta)
    x = _from_tokens(t, x)
    return x

_drawn_inputs = setup_inputs


def setup_inputs(seed=0):
    import zlib

    import numpy as np

    out = dict(_drawn_inputs(seed))
    spreads = {'L0_conv_ln_g': (1.0, 0.2),
     'L0_conv_ln_b': (0.0, 0.1),
     'L0_conv_bg': (1.0, 0.6),
     'L0_conv_bo': (0.0, 0.1),
     'L0_ffn_br': (0.0, 0.1),
     'L0_ffn_b1': (0.0, 0.394),
     'L0_ffn_b2': (0.0, 0.1),
     'L0_ffn_gamma': (1.0, 0.2),
     'L0_ffn_beta': (0.0, 0.1)}
    factors = {'L0_conv_Wg': 6.649, 'L0_ffn_Wr': 8.0}
    for name, (base, spread) in spreads.items():
        noise = np.random.default_rng([zlib.crc32(name.encode()), seed]).standard_normal(out[name].shape)
        drawn = base * np.exp(spread * noise) if base else spread * noise
        out[name] = jnp.asarray(drawn.astype(out[name].dtype))
    for name, factor in factors.items():
        out[name] = (out[name] * factor).astype(out[name].dtype)
    return out
```

```python
from contextlib import ExitStack

import concourse.bass as bass
from concourse import mybir

F32 = mybir.dt.float32
F16 = mybir.dt.float16
U32 = mybir.dt.uint32
ALU = mybir.AluOpType
ACT = mybir.ActivationFunctionType
AX = mybir.AxisListType.X

ROWS, TOK, DIM = 16, 128, 64
HEADS, HD = 8, 16
INNER = HEADS * HD
EXPERTS, HID = 8, 128
TOKENS = ROWS * TOK
CHUNK = 4
CHUNKS = ROWS // CHUNK
EPS_OUTER, EPS_LN = 1e-6, 1e-5
CAPACITY = float(-(-TOKENS * 5 // (4 * EXPERTS)))
WSCALE = 64.0
SLOT, STACK = HD, 4 * HD
SHIFT = 3 * HD
QK = HEADS * STACK
K_AT = QK + SLOT
VCOLS = 32
AHEAD = 4
UNROLL = 4


def metaformer_kernel(nc, x, ln_g, ln_b, Wq, Wkv, Wg, bg, Wo, bo, Wr, br, W1, b1, W2, b2, gamma, beta, out):
    x_d = x.rearrange("a s p d -> p (a s) d")
    out_d = out.rearrange("a s p d -> p (a s) d")
    ctx = ExitStack()
    with ctx:
        def sb(name, shape, dt=F32):
            return ctx.enter_context(nc.sbuf_tensor(name, shape, dt))

        def sem(name):
            return ctx.enter_context(nc.semaphore(name))

        x_all = sb("x_all", [TOK, ROWS, DIM])
        w_in = sb("w_in", [2 * DIM, 4 * INNER])
        w1_in = sb("w1_in", [2 * DIM, EXPERTS, HID])
        w2_in = sb("w2_in", [HID, EXPERTS, DIM])
        wo = sb("wo", [INNER, DIM])
        wr = sb("wr", [DIM, EXPERTS])
        br_row = sb("br_row", [1, EXPERTS])
        b1_t = sb("b1_t", [HID, EXPERTS])
        b2_t = sb("b2_t", [2 * DIM, EXPERTS])
        lng_b = sb("lng_b", [TOK, DIM])
        lnb_b = sb("lnb_b", [TOK, DIM])
        bo_b = sb("bo_b", [TOK, DIM])
        bg_b = sb("bg_b", [TOK, INNER])
        gamma_b = sb("gamma_b", [TOK, DIM])
        beta_b = sb("beta_b", [TOK, DIM])
        ident = sb("ident", [128, 128])
        ident16 = sb("ident16", [128, 128], F16)
        ones = sb("ones", [128, 128])
        neg_half = sb("neg_half", [TOK, ROWS])
        w_hi = sb("w_hi", [2 * DIM, 4 * INNER], F16)
        w_lo = sb("w_lo", [2 * DIM, 4 * INNER], F16)
        w1_split = sb("w1_split", [2 * DIM, 2, EXPERTS, HID], F16)
        stats = sb("stats", [TOK, CHUNK, 6])
        mv = sb("mv", [TOK, ROWS, 2])
        rstd = sb("rstd", [TOK, ROWS])
        xn = sb("xn", [TOK, ROWS, DIM])
        x_bo = sb("x_bo", [TOK, ROWS, DIM])
        x_split = sb("x_split", [TOK, ROWS, 2, DIM], F16)
        x_t = sb("x_t", [2 * DIM, ROWS, TOK], F16)
        qkvg = sb("qkvg", [TOK, 4, 4 * INNER])
        stack = sb("stack", [TOK, 4, 2 * (K_AT + 2 * SLOT)], F16)
        qk_t = sb("qk_t", [128, 2, 2, 4, TOK], F16)
        q2_t = sb("q2_t", [128, 2, 4, TOK], F16)
        v_aug = sb("v_aug", [TOK, 4, HEADS, VCOLS])
        gate = sb("gate", [TOK, 4, INNER])
        th = sb("th", [TOK, 4, INNER])
        prob = sb("prob", [TOK, 2, 2, 4, TOK])
        u_sb = sb("u_sb", [128, 2, 2, TOK])
        rden = sb("rden", [TOK, 4, HEADS])
        og1 = sb("og1", [TOK, 4, INNER])
        og = sb("og", [TOK, 4, INNER])
        og_t = sb("og_t", [INNER, 2, TOK])
        t_all = sb("t_all", [TOK, ROWS, DIM])
        mv2 = sb("mv2", [TOK, ROWS, 2])
        rstd2 = sb("rstd2", [TOK, ROWS])
        tn = sb("tn", [TOK, ROWS, DIM])
        tn_split = sb("tn_split", [TOK, ROWS, 2, DIM], F16)
        tn_t = sb("tn_t", [2 * DIM, ROWS, TOK], F16)
        tn_sum = sb("tn_sum", [TOK, DIM])
        mean_col = sb("mean_col", [DIM, 1])
        rt = sb("rt", [1, 16, EXPERTS])
        top_i = sb("top_i", [1, EXPERTS], U32)
        top_b = sb("top_b", [128, 2])
        w1_sel = sb("w1_sel", [2 * DIM, 2, 2, HID], F16)
        w2_sel = sb("w2_sel", [HID, 2, DIM])
        b1_sel = sb("b1_sel", [HID, 2])
        b2_part = sb("b2_part", [2 * DIM, 1])
        b2_sel = sb("b2_sel", [2 * DIM, 1])
        hid = sb("hid", [HID, 2, TOKENS])
        y_t = sb("y_t", [2 * DIM, 2, 4 * TOK])
        z = sb("z", [TOK, ROWS, DIM])
        zsum = sb("zsum", [TOK, ROWS])
        zc = sb("zc", [TOK, ROWS, DIM])
        zsq = sb("zsq", [TOK, ROWS, DIM])
        zvar = sb("zvar", [TOK, ROWS])
        zr = sb("zr", [TOK, ROWS])
        zn = sb("zn", [TOK, ROWS, DIM])
        zg = sb("zg", [TOK, ROWS, DIM])
        zb = sb("zb", [TOK, ROWS, DIM])
        res = sb("res", [TOK, ROWS, DIM])

        bank = [ctx.enter_context(nc.psum_tensor(f"bank{i}", [128, 512], F32)) for i in range(8)]
        B_PROJ, B_TQ, B_S1, B_S2, B_U, B_OUT = 0, 1, 2, 4, 6, 7
        proj_p = bank[B_PROJ][:, :]
        ogt_p = bank[B_PROJ][:, 0:TOK]
        tq_p = bank[B_TQ][:, :].bitcast(F16).rearrange("c (a p t) -> c a p t", a=2, p=4)
        s1_p = [bank[B_S1 + a][:, :].rearrange("q (p k) -> q p k", p=4) for a in range(2)]
        s2_p = [bank[B_S2 + a][:, :].rearrange("k (p q) -> k p q", p=4) for a in range(2)]
        u_p = bank[B_U][:, 0:2 * TOK].rearrange("c (a q) -> c a q", a=2)
        ut_p = bank[B_OUT][:, 0:2 * TOK].rearrange("q (h c) -> q h c", h=HEADS)
        y_p = bank[B_OUT][:, 2 * TOK:2 * TOK + DIM]

        ld = {n: sem(f"loaded_{n}") for n in ("x0", "x1", "x2", "x3", "w", "lng", "lnb", "bo", "bg", "wo",
                                              "w1", "w2", "b1", "b2", "wr", "br", "gamma", "beta")}
        pool_order = sem("pool_order")
        dve_order = sem("dve_order")
        consts = sem("consts")
        ident_ok = sem("ident_ok")
        buffers_ok = sem("buffers_ok")
        w_hi_ok = sem("w_hi_ok")
        w_lo_ok = sem("w_lo_ok")
        mv_ok = sem("mv_ok")
        rstd_ok = sem("rstd_ok")
        xn_ok = sem("xn_ok")
        x_split_ok = sem("x_split_ok")
        x_tp = sem("x_tp")
        x_t_ok = sem("x_t_ok")
        x_bo_ok = sem("x_bo_ok")
        proj_done = sem("proj_done")
        proj_copied = sem("proj_copied")
        hi_ok = sem("hi_ok")
        split_ok = sem("split_ok")
        v_ok = sem("v_ok")
        gate_ok = sem("gate_ok")
        tqk_done = sem("tqk_done")
        tqk_copied = sem("tqk_copied")
        s1_done = [sem("s1a_done"), sem("s1b_done")]
        max_done = sem("max_done")
        tq2_done = sem("tq2_done")
        tq2_copied = sem("tq2_copied")
        s2_done = [sem("s2a_done"), sem("s2b_done")]
        exp_done = sem("exp_done")
        tanh_done = sem("tanh_done")
        pv_done = sem("pv_done")
        u_copied = sem("u_copied")
        ut_done = sem("ut_done")
        ut_read = sem("ut_read")
        og_ok = sem("og_ok")
        ogt_done = sem("ogt_done")
        ogt_copied = sem("ogt_copied")
        wo_done = sem("wo_done")
        t_ok = sem("t_ok")
        mv2_ok = sem("mv2_ok")
        rstd2_ok = sem("rstd2_ok")
        tn_ok = sem("tn_ok")
        tn_split_ok = sem("tn_split_ok")
        tn_tp = sem("tn_tp")
        tn_t_ok = sem("tn_t_ok")
        w1_split_ok = sem("w1_split_ok")
        sum_ok = sem("sum_ok")
        mean_done = sem("mean_done")
        mean_ok = sem("mean_ok")
        logits_done = sem("logits_done")
        r_max = sem("r_max")
        r_exp = sem("r_exp")
        topw_ok = sem("topw_ok")
        topb_done = sem("topb_done")
        w1_sel_ok = sem("w1_sel_ok")
        b1_sel_ok = sem("b1_sel_ok")
        w2_sel_ok = sem("w2_sel_ok")
        b2_sel_ok = sem("b2_sel_ok")
        fc1_done = sem("fc1_done")
        gelu_done = sem("gelu_done")
        fc2_done = sem("fc2_done")
        y_copied = sem("y_copied")
        yt_done = sem("yt_done")
        z_ok = sem("z_ok")
        zsum_ok = sem("zsum_ok")
        zc_ok = sem("zc_ok")
        zsq_ok = sem("zsq_ok")
        zvar_ok = sem("zvar_ok")
        zr_ok = sem("zr_ok")
        zn_ok = sem("zn_ok")
        res_ok = sem("res_ok")
        stored = sem("stored")

        block = ctx.enter_context(nc.Block())

        def on(stage, t):
            return not isinstance(t, int) or 0 <= t - stage < ROWS

        def steps(engine, step, before=None, after=None):
            for t in range(AHEAD):
                step(t, t)
                if before is not None:
                    before(t)
            if LOOP:
                with engine.Fori(AHEAD, ROWS, UNROLL) as t:
                    for k in range(UNROLL):
                        step(t + k, k)
            else:
                for t in range(AHEAD, ROWS):
                    step(t, t % 4)
            for t in range(ROWS, ROWS + AHEAD):
                if after is not None:
                    after(t - ROWS)
                step(t, t % 4)

        def stack_slots(b, q_slot, k_slot):
            first = q_slot * SLOT
            apart = K_AT + (k_slot - q_slot) * SLOT
            v = stack[:, b, first:first + 2 * apart].rearrange("t (a c) -> t a c", a=2)
            return v[:, :, 0:QK].rearrange("t a (h c) -> t a h c", c=STACK)[:, :, :, 0:SLOT]

        def pair(b, which, p):
            first = which * K_AT + 2 * STACK * p
            return stack[:, b, first:first + 2 * STACK]

        @block.sync
        def _(sp):
            for c in range(CHUNKS):
                sp.dma_start(x_all[:, c * CHUNK:(c + 1) * CHUNK, :],
                             x_d[:, c * CHUNK:(c + 1) * CHUNK, :]).then_inc(ld[f"x{c}"], 16)
                if c == 0:
                    for half in range(2):
                        rows = slice(half * DIM, (half + 1) * DIM)
                        sp.dma_start(w_in[rows, 0:INNER], Wq).then_inc(ld["w"], 16)
                        sp.dma_start(w_in[rows, INNER:3 * INNER], Wkv).then_inc(ld["w"], 16)
                        sp.dma_start(w_in[rows, 3 * INNER:4 * INNER], Wg).then_inc(ld["w"], 16)
            for half in range(2):
                rows = slice(half * DIM, (half + 1) * DIM)
                sp.dma_start(w1_in[rows, :, :], W1.rearrange("e d f -> d e f")).then_inc(ld["w1"], 16)
                sp.dma_start(b2_t[rows, :], b2).then_inc(ld["b2"], 16)
            sp.dma_start(wo[:, :], Wo).then_inc(ld["wo"], 16)
            sp.dma_start(w2_in[:, :, :], W2.rearrange("e f d -> f e d")).then_inc(ld["w2"], 16)
            sp.dma_start(b1_t[:, :], b1).then_inc(ld["b1"], 16)
            sp.dma_start(wr[:, :], Wr).then_inc(ld["wr"], 16)
            sp.dma_start(br_row[0:1, :], br.rearrange("(a e) -> a e", a=1)).then_inc(ld["br"], 16)
            for c in range(2):
                sp.wait_ge(res_ok, c + 1)
                sp.dma_start(out_d[:, 8 * c:8 * c + 8, :], res[:, 8 * c:8 * c + 8, :]).then_inc(stored, 16)
            sp.wait_ge(stored, 32)

        @block.scalar
        def _(act):
            def bcast(v):
                return v.rearrange("(a d) -> a d", a=1).broadcast_to([TOK, v.shape[0]])

            for name, dst, src in (("lng", lng_b, ln_g), ("lnb", lnb_b, ln_b), ("bo", bo_b, bo),
                                   ("bg", bg_b, bg), ("gamma", gamma_b, gamma), ("beta", beta_b, beta)):
                act.dma_start(dst[:, :], bcast(src)).then_inc(ld[name], 16)
            act.wait_ge(ld["w"], 96)
            nc.scalar.activation(w_hi[:, :], w_in[:, :], ACT.Copy, scale=WSCALE).then_inc(w_hi_ok, 1)

            def copy_x_t(c):
                act.wait_ge(x_tp, c + 1)
                nc.scalar.activation(x_t[:, c * CHUNK:(c + 1) * CHUNK, :],
                                     bank[B_U][:, 0:256].bitcast(F16).rearrange("c (s t) -> c s t", s=CHUNK),
                                     ACT.Copy).then_inc(x_t_ok, 1)

            def step(t, k):
                if on(3, t):
                    s, b = t - 3, (k - 3) % 2
                    for a in range(2):
                        act.wait_ge(s2_done[a], s + 1)
                        if on(5, t):
                            act.wait_ge(pv_done, s - 1)
                        nc.scalar.activation(prob[:, b, a], s2_p[a], ACT.Exp, scale=HD ** -0.5).then_inc(exp_done, 1)
                if on(0, t):
                    s, b = t, k
                    act.wait_ge(proj_done, s + 1)
                    if on(4, t):
                        act.wait_ge(split_ok, s - 3)
                        act.wait_ge(v_ok, s - 3)
                        act.wait_ge(gate_ok, s - 3)
                    nc.scalar.activation(qkvg[:, b, :], proj_p, ACT.Copy, scale=1 / WSCALE).then_inc(proj_copied, 1)
                if on(1, t):
                    s, b = t - 1, (k - 1) % 4
                    act.wait_ge(gate_ok, s + 1)
                    if on(5, t):
                        act.wait_ge(ut_read, s - 3)
                    nc.scalar.activation(th[:, b, :], gate[:, b, :], ACT.Tanh, scale=0.5).then_inc(tanh_done, 1)
                if on(3, t):
                    s, b = t - 3, (k - 3) % 2
                    act.wait_ge(pv_done, s + 1)
                    if on(5, t):
                        act.wait_ge(ut_done, s - 1)
                    nc.scalar.activation(u_sb[:, b], u_p, ACT.Copy).then_inc(u_copied, 1)
                if on(4, t):
                    s, b = t - 4, k % 2
                    act.wait_ge(ogt_done, s + 1)
                    if on(6, t):
                        act.wait_ge(wo_done, s - 1)
                    nc.scalar.activation(og_t[:, b, :], ogt_p, ACT.Copy).then_inc(ogt_copied, 1)

            copy_x_t(0)
            steps(act, step, before=lambda c: copy_x_t(c + 1) if c + 1 < CHUNKS else None)

            for c in range(CHUNKS):
                act.wait_ge(tn_tp, c + 1)
                nc.scalar.activation(tn_t[:, c * CHUNK:(c + 1) * CHUNK, :],
                                     bank[B_S1 + c][:, 0:256].bitcast(F16).rearrange("c (s t) -> c s t", s=CHUNK),
                                     ACT.Copy).then_inc(tn_t_ok, 1)
            for n, (src, dst, width) in enumerate(((0, 1, EXPERTS), (4, 5, EXPERTS), (8, 9, 2))):
                act.wait_ge(r_max, n + 1)
                nc.scalar.activation(rt[0:1, dst, 0:width], rt[0:1, src, 0:width], ACT.Exp,
                                     bias=rt[0:1, 12, n:n + 1], accum_out=rt[0:1, 13, n:n + 1]).then_inc(r_exp, 1)
            act.wait_ge(b1_sel_ok, 1)
            for c in range(CHUNKS):
                for j in range(2):
                    n = 2 * c + j
                    act.wait_ge(fc1_done, n + 1)
                    nc.scalar.activation(hid[:, j, c * 512:(c + 1) * 512], bank[n][:, :], ACT.Gelu,
                                         bias=b1_sel[:, j:j + 1], scale=1 / WSCALE).then_inc(gelu_done, 1)
                if c % 2 == 1:
                    act.wait_ge(b2_sel_ok, 1)
                    act.wait_ge(fc2_done, c // 2 + 1)
                    nc.scalar.activation(y_t[:, c // 2, :], bank[c // 2][:, :], ACT.Identity,
                                         bias=b2_sel[:, 0:1]).then_inc(y_copied, 1)
            for c in range(2):
                r = slice(8 * c, 8 * c + 8)
                act.wait_ge(zc_ok, c + 1)
                nc.scalar.activation(zsq[:, r, :], zc[:, r, :], ACT.Square).then_inc(zsq_ok, 1)

        @block.vector
        def _(dve):
            order = [0]

            def then_next(instruction):
                order[0] += 1
                instruction.then_inc(dve_order, 1)
                dve.wait_ge(dve_order, order[0])

            nc.vector.memset(ones[:, :], 1.0).then_inc(consts, 1)
            nc.vector.memset(neg_half[:, :], -0.5).then_inc(consts, 1)

            def norm(c, src, mv_, rstd_, dst, read_ok, mv_sem, rstd_sem, dst_sem):
                read_ok(c)
                for i in range(CHUNK):
                    last = nc.vector.bn_stats(stats[:, i, :], src[:, c * CHUNK + i, :])
                then_next(last)
                for i in range(CHUNK):
                    last = nc.vector.bn_aggr(mv_[:, c * CHUNK + i, :], stats[:, i, :])
                last.then_inc(mv_sem, 1)
                dve.wait_ge(rstd_sem, c + 1)
                for i in range(CHUNK):
                    s = c * CHUNK + i
                    last = nc.vector.tensor_scalar(dst[:, s, :], src[:, s, :], mv_[:, s, 0:1], rstd_[:, s:s + 1],
                                                   ALU.subtract, ALU.mult)
                last.then_inc(dst_sem, 1)

            def norm_x(c):
                norm(c, x_all, mv, rstd, xn, lambda c: dve.wait_ge(ld[f"x{c}"], 16), mv_ok, rstd_ok, xn_ok)

            def norm_t(c):
                norm(c, t_all, mv2, rstd2, tn, lambda c: dve.wait_ge(t_ok, (c + 1) * CHUNK), mv2_ok, rstd2_ok, tn_ok)

            norm_x(0)
            dve.wait_ge(w_hi_ok, 1)
            nc.vector.scalar_tensor_tensor(out=w_lo[:, :], in0=w_in[:, :], scalar=WSCALE, in1=w_hi[:, :],
                                           op0=ALU.mult, op1=ALU.subtract).then_inc(w_lo_ok, 1)
            dve.wait_ge(buffers_ok, 1)

            def step(t, k):
                if on(1, t):
                    s, b = t - 1, (k - 1) % 2
                    dve.wait_ge(tqk_done, s + 1)
                    if on(3, t):
                        dve.wait_ge(s2_done[1], s - 1)
                    nc.vector.tensor_copy(qk_t[:, b], tq_p).then_inc(tqk_copied, 1)
                if on(3, t):
                    s, b = t - 3, (k - 3) % 4
                    dve.wait_ge(ut_done, s + 1)
                    dve.wait_ge(tanh_done, s + 1)
                    if on(7, t):
                        dve.wait_ge(og_ok, s - 3)
                    nc.vector.reciprocal(rden[:, b, :], ut_p[:, :, HD])
                    nc.vector.scalar_tensor_tensor(out=og1[:, b, :].rearrange("t (h c) -> t h c", h=HEADS),
                                                   in0=th[:, b, :].rearrange("t (h c) -> t h c", h=HEADS), scalar=1.0,
                                                   in1=ut_p[:, :, 0:HD], op0=ALU.add, op1=ALU.mult).then_inc(ut_read, 1)
                if on(1, t):
                    s, b = t - 1, (k - 1) % 4
                    for a in range(2):
                        dve.wait_ge(s1_done[a], s + 1)
                        q = stack[:, b, 0:QK].rearrange("t (p a c) -> t p a c", p=4, a=2)
                        nc.vector.tensor_reduce(q[:, :, a, SHIFT], s1_p[a], AX, ALU.max, negate=True).then_inc(max_done, 1)
                if on(2, t):
                    s, b = t - 2, (k - 2) % 2
                    dve.wait_ge(tq2_done, s + 1)
                    if on(4, t):
                        dve.wait_ge(s2_done[1], s - 1)
                    nc.vector.tensor_copy(q2_t[:, b], tq_p[:, 0]).then_inc(tq2_copied, 1)
                if on(4, t):
                    s = t - 4
                    dve.wait_ge(wo_done, s + 1)
                    if isinstance(t, int):
                        dve.wait_ge(x_bo_ok, s // CHUNK + 1)
                        nc.vector.tensor_tensor(t_all[:, s, :], y_p, x_bo[:, s, :], ALU.add).then_inc(t_ok, 1)
                    else:
                        nc.vector.tensor_tensor(t_all[:, bass.ds(s, 1), :].rearrange("t s d -> t (s d)"), y_p,
                                                x_bo[:, bass.ds(s, 1), :].rearrange("t s d -> t (s d)"),
                                                ALU.add).then_inc(t_ok, 1)

            steps(dve, step, before=lambda c: norm_x(c + 1) if c + 1 < CHUNKS else dve.wait_ge(x_bo_ok, CHUNKS),
                  after=lambda c: norm_t(c) if c + 1 < CHUNKS else None)
            norm_t(CHUNKS - 1)

            dve.wait_ge(mean_done, 1)
            nc.vector.tensor_scalar(mean_col[:, :], bank[0][0:DIM, 0:1], 1.0 / TOKENS, None, ALU.mult).then_inc(mean_ok, 1)
            dve.wait_ge(logits_done, 1)
            dve.wait_ge(ld["br"], 16)
            then_next(nc.vector.tensor_tensor(rt[0:1, 0, :], bank[1][0:1, 0:EXPERTS], br_row[0:1, :], ALU.add))
            nc.vector.tensor_reduce(rt[0:1, 12, 0:1], rt[0:1, 0, :], AX, ALU.max, negate=True).then_inc(r_max, 1)
            dve.wait_ge(r_exp, 1)
            then_next(nc.vector.reciprocal(rt[0:1, 14, 0:1], rt[0:1, 13, 0:1]))
            then_next(nc.vector.tensor_scalar(rt[0:1, 2, :], rt[0:1, 1, :], rt[0:1, 14, 0:1], None, ALU.mult))
            then_next(nc.vector.tensor_scalar(rt[0:1, 3, :], rt[0:1, 2, :], float(TOKENS), None, ALU.mult))
            then_next(nc.vector.reciprocal(rt[0:1, 6, :], rt[0:1, 3, :]))
            then_next(nc.vector.tensor_scalar(rt[0:1, 7, :], rt[0:1, 6, :], CAPACITY, 1.0, ALU.mult, ALU.min))
            then_next(nc.vector.tensor_tensor(rt[0:1, 4, :], rt[0:1, 2, :], rt[0:1, 7, :], ALU.mult))
            nc.vector.tensor_reduce(rt[0:1, 12, 1:2], rt[0:1, 4, :], AX, ALU.max, negate=True).then_inc(r_max, 1)
            dve.wait_ge(r_exp, 2)
            then_next(nc.vector.reciprocal(rt[0:1, 14, 1:2], rt[0:1, 13, 1:2]))
            then_next(nc.vector.tensor_scalar(rt[0:1, 10, :], rt[0:1, 5, :], rt[0:1, 14, 1:2], None, ALU.mult))
            then_next(nc.vector.max(rt[0:1, 8, :], rt[0:1, 10, :]))
            nc.vector.tensor_scalar(rt[0:1, 12, 2:3], rt[0:1, 8, 0:1], -1.0, None, ALU.mult).then_inc(r_max, 1)
            then_next(nc.vector.max_index(top_i[0:1, :], rt[0:1, 8, :], rt[0:1, 10, :]))
            expert = [dve.value_load(top_i[0:1, j:j + 1], min_val=0, max_val=EXPERTS - 1) for j in range(2)]
            dve.wait_ge(w1_split_ok, 1)
            for j in range(2):
                nc.vector.tensor_copy(w1_sel[:, j], w1_split[:, :, bass.ds(expert[j], 1), :].rearrange(
                    "c l e f -> c l (e f)")).then_inc(w1_sel_ok, 1)
            dve.wait_ge(ld["b1"], 16)
            for j in range(2):
                last = nc.vector.tensor_copy(b1_sel[:, j:j + 1], b1_t[:, bass.ds(expert[j], 1)])
            last.then_inc(b1_sel_ok, 1)
            dve.wait_ge(r_exp, 3)
            then_next(nc.vector.reciprocal(rt[0:1, 14, 2:3], rt[0:1, 13, 2:3]))
            nc.vector.tensor_scalar(rt[0:1, 11, 0:2], rt[0:1, 9, 0:2], rt[0:1, 14, 2:3], None, ALU.mult).then_inc(topw_ok, 1)
            dve.wait_ge(topb_done, 1)
            then_next(nc.vector.tensor_copy(top_b[:, :], bank[2][:, 0:2]))
            dve.wait_ge(ld["w2"], 16)
            for j in range(2):
                nc.vector.tensor_scalar(w2_sel[:, j, :], w2_in[:, bass.ds(expert[j], 1), :].rearrange("f e d -> f (e d)"),
                                        top_b[:, j:j + 1], None, ALU.mult).then_inc(w2_sel_ok, 1)
            dve.wait_ge(ld["b2"], 32)
            then_next(nc.vector.tensor_scalar(b2_part[:, :], b2_t[:, bass.ds(expert[0], 1)], top_b[:, 0:1], None, ALU.mult))
            nc.vector.scalar_tensor_tensor(out=b2_sel[:, :], in0=b2_t[:, bass.ds(expert[1], 1)], scalar=top_b[:, 1:2],
                                           in1=b2_part[:, :], op0=ALU.mult, op1=ALU.add).then_inc(b2_sel_ok, 1)

            for c in range(2):
                r = slice(8 * c, 8 * c + 8)
                dve.wait_ge(yt_done, c + 1)
                then_next(nc.vector.tensor_tensor(
                    z[:, r, :].rearrange("t (h i) d -> t i h d", h=2),
                    bank[6 + c][:, :].rearrange("t (i h d) -> t i h d", i=4, h=2),
                    tn[:, r, :].rearrange("t (h i) d -> t i h d", h=2), ALU.add))
                then_next(nc.vector.tensor_reduce(zsum[:, r], z[:, r, :], AX, ALU.add))
                nc.vector.scalar_tensor_tensor(out=zc[:, r, :], in0=zsum[:, r].unsqueeze(2).broadcast_to([TOK, 8, DIM]),
                                               scalar=-1.0 / DIM, in1=z[:, r, :], op0=ALU.mult,
                                               op1=ALU.add).then_inc(zc_ok, 1)
            for c in range(2):
                r = slice(8 * c, 8 * c + 8)
                dve.wait_ge(zsq_ok, c + 1)
                nc.vector.tensor_reduce(zvar[:, r], zsq[:, r, :], AX, ALU.add).then_inc(zvar_ok, 1)
                dve.wait_ge(zr_ok, c + 1)
                nc.vector.tensor_tensor(zn[:, r, :], zc[:, r, :], zr[:, r].unsqueeze(2).broadcast_to([TOK, 8, DIM]),
                                        ALU.mult).then_inc(zn_ok, 1)

        @block.gpsimd
        def _(pool):
            order = [0]

            def then_next(instruction):
                order[0] += 1
                instruction.then_inc(pool_order, 1)
                pool.wait_ge(pool_order, order[0])

            pool.wait_ge(consts, 2)
            nc.gpsimd.affine_select(out=ident[:, :], in_=ones[:, :], compare_op=ALU.is_equal, fill=0.0, base=0,
                                    pattern=[[-1, 128]], channel_multiplier=1).then_inc(ident_ok, 1)
            pool.wait_ge(ident_ok, 1)
            nc.gpsimd.tensor_copy(ident16[:, :], ident[:, :]).then_inc(ident_ok, 1)

            def power(c, mv_, rstd_, scale, eps, mv_sem, rstd_sem):
                r = slice(c * CHUNK, (c + 1) * CHUNK)
                pool.wait_ge(mv_sem, c + 1)
                then_next(nc.gpsimd.tensor_scalar(rstd_[:, r], mv_[:, r, 1], scale, eps, ALU.mult, ALU.add))
                nc.gpsimd.tensor_tensor(rstd_[:, r], rstd_[:, r], neg_half[:, r], ALU.pow).then_inc(rstd_sem, 1)

            def finish_x(c):
                r = slice(c * CHUNK, (c + 1) * CHUNK)
                power(c, mv, rstd, 1.0 + EPS_LN, EPS_LN * EPS_OUTER, mv_ok, rstd_ok)
                pool.wait_ge(xn_ok, c + 1)
                pool.wait_ge(ld["lng"], 16)
                pool.wait_ge(ld["lnb"], 16)
                wide = [TOK, CHUNK, DIM]
                then_next(nc.gpsimd.tensor_tensor(xn[:, r, :], xn[:, r, :], lng_b[:, :].unsqueeze(1).broadcast_to(wide), ALU.mult))
                then_next(nc.gpsimd.tensor_tensor(xn[:, r, :], xn[:, r, :], lnb_b[:, :].unsqueeze(1).broadcast_to(wide), ALU.add))
                then_next(nc.gpsimd.tensor_copy(x_split[:, r, 0, :], xn[:, r, :]))
                nc.gpsimd.tensor_tensor(x_split[:, r, 1, :], xn[:, r, :], x_split[:, r, 0, :], ALU.subtract).then_inc(x_split_ok, 1)
                pool.wait_ge(ld["bo"], 16)
                nc.gpsimd.tensor_tensor(x_bo[:, r, :], x_all[:, r, :], bo_b[:, :].unsqueeze(1).broadcast_to(wide),
                                        ALU.add).then_inc(x_bo_ok, 1)

            def finish_t(c):
                r = slice(c * CHUNK, (c + 1) * CHUNK)
                power(c, mv2, rstd2, 1.0, EPS_LN, mv2_ok, rstd2_ok)
                pool.wait_ge(tn_ok, c + 1)
                for i in range(CHUNK):
                    then_next(nc.gpsimd.tensor_tensor(tn_sum[:, :], tn_sum[:, :], tn[:, c * CHUNK + i, :], ALU.add))
                if c == CHUNKS - 1:
                    pool.sem_inc(sum_ok, 1)
                then_next(nc.gpsimd.tensor_copy(tn_split[:, r, 0, :], tn[:, r, :]))
                nc.gpsimd.tensor_tensor(tn_split[:, r, 1, :], tn[:, r, :], tn_split[:, r, 0, :], ALU.subtract).then_inc(tn_split_ok, 1)

            finish_x(0)
            nc.gpsimd.memset(stack[:, :, :], 0.0)
            nc.gpsimd.memset(v_aug[:, :, :, HD:VCOLS], 0.0)
            then_next(nc.gpsimd.memset(tn_sum[:, :], 0.0))
            nc.gpsimd.memset(stack[:, :, K_AT:K_AT + QK].rearrange("t b (h c) -> t b h c", c=STACK)[:, :, :, SHIFT], 1.0)
            then_next(nc.gpsimd.memset(v_aug[:, :, :, HD], 2.0))
            pool.sem_inc(buffers_ok, 1)
            pool.wait_ge(ld["bg"], 16)

            def step(t, k):
                if on(0, t):
                    s, b = t, k
                    qk = qkvg[:, b, 0:2 * INNER].rearrange("t (a h c) -> t a h c", a=2, h=HEADS)
                    pool.wait_ge(proj_copied, s + 1)
                    if on(4, t):
                        pool.wait_ge(tq2_done, s - 3)
                    nc.gpsimd.tensor_copy(stack_slots(b, 0, 0), qk).then_inc(hi_ok, 1)
                    nc.gpsimd.tensor_copy(stack_slots(b, 1, 2), qk)
                    pool.wait_ge(hi_ok, s + 1)
                    nc.gpsimd.tensor_tensor(stack_slots(b, 2, 1), qk, stack_slots(b, 0, 0), ALU.subtract).then_inc(split_ok, 1)
                    if on(4, t):
                        pool.wait_ge(pv_done, s - 3)
                    nc.gpsimd.tensor_copy(v_aug[:, b, :, 0:HD], qkvg[:, b, 2 * INNER:3 * INNER].rearrange(
                        "t (h c) -> t h c", h=HEADS)).then_inc(v_ok, 1)
                    if on(4, t):
                        pool.wait_ge(tanh_done, s - 3)
                    nc.gpsimd.tensor_tensor(gate[:, b, :], qkvg[:, b, 3 * INNER:4 * INNER], bg_b[:, :],
                                            ALU.add).then_inc(gate_ok, 1)
                if on(3, t):
                    s, b = t - 3, (k - 3) % 4
                    pool.wait_ge(ut_read, s + 1)
                    if on(7, t):
                        pool.wait_ge(ogt_done, s - 3)
                    nc.gpsimd.tensor_tensor(og[:, b, :].rearrange("t (h c) -> t h c", h=HEADS),
                                            og1[:, b, :].rearrange("t (h c) -> t h c", h=HEADS),
                                            rden[:, b, :].unsqueeze(2).broadcast_to([TOK, HEADS, HD]),
                                            ALU.mult).then_inc(og_ok, 1)

            def before(c):
                if c + 1 < CHUNKS:
                    finish_x(c + 1)
                else:
                    pool.wait_ge(ld["w1"], 32)
                    then_next(nc.gpsimd.tensor_scalar(w1_split[:, 0], w1_in[:, :, :], WSCALE, None, ALU.mult))
                    then_next(nc.gpsimd.tensor_scalar(w1_in[:, :, :], w1_in[:, :, :], WSCALE, None, ALU.mult))
                    nc.gpsimd.tensor_tensor(w1_split[:, 1], w1_in[:, :, :], w1_split[:, 0], ALU.subtract).then_inc(w1_split_ok, 1)

            steps(pool, step, before=before, after=lambda c: finish_t(c) if c + 1 < CHUNKS else None)
            finish_t(CHUNKS - 1)

            for c in range(2):
                r = slice(8 * c, 8 * c + 8)
                pool.wait_ge(zvar_ok, c + 1)
                then_next(nc.gpsimd.tensor_scalar(zr[:, r], zvar[:, r], 1.0 / DIM, EPS_LN, ALU.mult, ALU.add))
                nc.gpsimd.tensor_tensor(zr[:, r], zr[:, r], neg_half[:, r], ALU.pow).then_inc(zr_ok, 1)
                pool.wait_ge(zn_ok, c + 1)
                wide = [TOK, 8, DIM]
                pool.wait_ge(ld["gamma"], 16)
                then_next(nc.gpsimd.tensor_tensor(zg[:, r, :], zn[:, r, :], gamma_b[:, :].unsqueeze(1).broadcast_to(wide), ALU.mult))
                pool.wait_ge(ld["beta"], 16)
                then_next(nc.gpsimd.tensor_tensor(zb[:, r, :], zg[:, r, :], beta_b[:, :].unsqueeze(1).broadcast_to(wide), ALU.add))
                nc.gpsimd.tensor_tensor(res[:, r, :], zb[:, r, :], t_all[:, r, :], ALU.add).then_inc(res_ok, 1)

        @block.tensor
        def _(pe):
            pe.wait_ge(ident_ok, 2)

            def transpose_x(c):
                pe.wait_ge(x_split_ok, c + 1)
                if c > 0:
                    pe.wait_ge(x_t_ok, c)
                dst = bank[B_U][:, 0:256].bitcast(F16)
                for i in range(CHUNK):
                    last = nc.tensor.transpose(dst[:, i * TOK:(i + 1) * TOK],
                                               x_split[:, c * CHUNK + i].rearrange("t l d -> t (l d)"), ident16[:, :])
                last.then_inc(x_tp, 1)

            def step(t, k):
                if on(0, t):
                    s = t
                    if isinstance(t, int):
                        pe.wait_ge(x_t_ok, s // CHUNK + 1)
                        lhs = x_t[:, s, :]
                    else:
                        lhs = x_t[:, bass.ds(s, 1), :].rearrange("c s t -> c (s t)")
                    if on(1, t):
                        pe.wait_ge(proj_copied, s)
                    if on(5, t):
                        pe.wait_ge(ogt_copied, s - 4)
                    nc.tensor.matmul(proj_p, lhs, w_hi[:, :], start=True, stop=False)
                    nc.tensor.matmul(proj_p, lhs, w_lo[:, :], start=False, stop=True).then_inc(proj_done, 1)
                if on(1, t):
                    s, b = t - 1, (k - 1) % 4
                    pe.wait_ge(split_ok, s + 1)
                    if on(3, t):
                        pe.wait_ge(tq2_copied, s - 1)
                    for which in range(2):
                        for p in range(4):
                            last = nc.tensor.transpose(tq_p[:, which, p, :], pair(b, which, p), ident16[:, :])
                    last.then_inc(tqk_done, 1)
                if on(3, t):
                    s, b, b2_ = t - 3, (k - 3) % 4, (k - 3) % 2
                    pe.wait_ge(exp_done, 2 * s + 2)
                    pe.wait_ge(v_ok, s + 1)
                    if on(4, t):
                        pe.wait_ge(u_copied, s)
                    else:
                        pe.wait_ge(x_t_ok, CHUNKS)
                    for a in range(2):
                        for p in range(4):
                            last = nc.tensor.matmul(u_p[32 * p:32 * p + 32, a, :], v_aug[:, b, 2 * p + a, :],
                                                    prob[:, b2_, a, p, :], start=True, stop=True)
                    last.then_inc(pv_done, 1)
                if on(4, t):
                    s, b = t - 4, k % 4
                    pe.wait_ge(og_ok, s + 1)
                    if on(0, t):
                        pe.wait_ge(proj_copied, t + 1)
                    elif s > 0:
                        pe.wait_ge(ogt_copied, s)
                    nc.tensor.transpose(ogt_p, og[:, b, :], ident[:, :]).then_inc(ogt_done, 1)
                if on(1, t):
                    s, b = t - 1, (k - 1) % 2
                    pe.wait_ge(tqk_copied, s + 1)
                    if on(2, t):
                        pe.wait_ge(max_done, 2 * s)
                    for p in range(4):
                        for a in range(2):
                            r = slice(64 * a, 64 * a + SHIFT)
                            last = nc.tensor.matmul(s1_p[a][:, p, :], qk_t[r, b, 0, p, :], qk_t[r, b, 1, p, :],
                                                    start=True, stop=True)
                            if p == 3:
                                last.then_inc(s1_done[a], 1)
                if on(3, t):
                    s, b = t - 3, (k - 3) % 2
                    pe.wait_ge(u_copied, s + 1)
                    if on(4, t):
                        pe.wait_ge(ut_read, s)
                    if on(5, t):
                        pe.wait_ge(t_ok, s - 1)
                    for a in range(2):
                        last = nc.tensor.transpose(ut_p.rearrange("q (p a) c -> q p a c", a=2)[:, :, a, :], u_sb[:, b, a, :], ident[:, :])
                    last.then_inc(ut_done, 1)
                if on(2, t):
                    s, b = t - 2, (k - 2) % 4
                    pe.wait_ge(max_done, 2 * s + 2)
                    if on(1, t):
                        pe.wait_ge(tqk_copied, t)
                    else:
                        pe.wait_ge(tq2_copied, s)
                    for p in range(4):
                        last = nc.tensor.transpose(tq_p[:, 0, p, :], pair(b, 0, p), ident16[:, :])
                    last.then_inc(tq2_done, 1)
                if on(4, t):
                    s, b = t - 4, k % 2
                    pe.wait_ge(ogt_copied, s + 1)
                    if on(3, t):
                        pe.wait_ge(ut_read, t - 2)
                    elif s > 0:
                        pe.wait_ge(t_ok, s)
                    nc.tensor.matmul(y_p, og_t[:, b, :], wo[:, :], start=True, stop=True).then_inc(wo_done, 1)
                if on(2, t):
                    s, b = t - 2, (k - 2) % 2
                    pe.wait_ge(tq2_copied, s + 1)
                    if on(3, t):
                        pe.wait_ge(exp_done, 2 * s)
                    for p in range(4):
                        for a in range(2):
                            r = slice(64 * a, 64 * a + STACK)
                            last = nc.tensor.matmul(s2_p[a][:, p, :], qk_t[r, b, 1, p, :], q2_t[r, b, p, :],
                                                    start=True, stop=True)
                            if p == 3:
                                last.then_inc(s2_done[a], 1)

            transpose_x(0)
            pe.wait_ge(w_hi_ok, 1)
            pe.wait_ge(w_lo_ok, 1)
            pe.wait_ge(buffers_ok, 1)
            pe.wait_ge(ld["wo"], 16)

            def before(c):
                if c + 1 < CHUNKS:
                    transpose_x(c + 1)

            steps(pe, step, before=before)

            pe.wait_ge(exp_done, 2 * ROWS)
            for c in range(CHUNKS):
                pe.wait_ge(tn_split_ok, c + 1)
                dst = bank[B_S1 + c][:, 0:256].bitcast(F16)
                for i in range(CHUNK):
                    last = nc.tensor.transpose(dst[:, i * TOK:(i + 1) * TOK],
                                               tn_split[:, c * CHUNK + i].rearrange("t l d -> t (l d)"), ident16[:, :])
                last.then_inc(tn_tp, 1)
            pe.wait_ge(sum_ok, 1)
            pe.wait_ge(ogt_copied, ROWS)
            nc.tensor.matmul(bank[0][0:DIM, 0:1], tn_sum[:, :], ones[:, 0:1], start=True, stop=True).then_inc(mean_done, 1)
            pe.wait_ge(mean_ok, 1)
            pe.wait_ge(ld["wr"], 16)
            nc.tensor.matmul(bank[1][0:1, 0:EXPERTS], mean_col[:, :], wr[:, :], start=True, stop=True).then_inc(logits_done, 1)
            pe.wait_ge(tn_t_ok, CHUNKS)
            pe.wait_ge(topw_ok, 1)
            nc.tensor.matmul(bank[2][:, 0:2], ones[0:1, :], rt[0:1, 11, 0:2], start=True, stop=True).then_inc(topb_done, 1)

            def fc1(c):
                for j in range(2):
                    n = 2 * c + j
                    if c == 0:
                        pe.wait_ge(w1_sel_ok, j + 1)
                    for part in range(2):
                        last = nc.tensor.matmul(bank[n][:, :], w1_sel[:, j, part, :],
                                                tn_t[:, c * CHUNK:(c + 1) * CHUNK, :].rearrange("c s t -> c (s t)"),
                                                start=part == 0, stop=part == 1)
                    last.then_inc(fc1_done, 1)

            def fc2(c):
                half = slice(DIM * (c % 2), DIM * (c % 2) + DIM)
                for j in range(2):
                    if c == 0:
                        pe.wait_ge(w2_sel_ok, j + 1)
                    pe.wait_ge(gelu_done, 2 * c + j + 1)
                    last = nc.tensor.matmul(bank[c // 2][half, :], w2_sel[:, j, :], hid[:, j, c * 512:(c + 1) * 512],
                                            start=j == 0, stop=j == 1)
                if c % 2 == 1:
                    last.then_inc(fc2_done, 1)

            pe.wait_ge(b2_sel_ok, 1)
            for c in range(CHUNKS):
                fc1(c)
            for c in range(CHUNKS):
                fc2(c)
                if c % 2 == 1:
                    i = c // 2
                    pe.wait_ge(y_copied, i + 1)
                    if True:
                        pe.wait_ge(gelu_done, 8)
                    for n in range(4):
                        last = nc.tensor.transpose(bank[6 + i][:, n * TOK:(n + 1) * TOK],
                                                   y_t[:, i, n * TOK:(n + 1) * TOK], ident[:, :])
                    last.then_inc(yt_done, 1)


LOOP = False

_ORDER = ["x", "L0_conv_ln_g", "L0_conv_ln_b", "L0_conv_Wq", "L0_conv_Wkv", "L0_conv_Wg", "L0_conv_bg", "L0_conv_Wo",
          "L0_conv_bo", "L0_ffn_Wr", "L0_ffn_br", "L0_ffn_W1", "L0_ffn_b1", "L0_ffn_W2", "L0_ffn_b2", "L0_ffn_gamma",
          "L0_ffn_beta"]

_COLUMNS = ("L0_ffn_b1", "L0_ffn_b2")


def kernel(**inputs):
    import numpy as _np
    import concourse.bacc as _bacc
    from concourse import mybir as _mybir
    from concourse.bass_utils import run_bass_kernel_spmd as _run

    nc = _bacc.Bacc("TRN2", target_bir_lowering=False, num_devices=1)
    arrays, args = {}, []
    for name in _ORDER:
        a = _np.asarray(inputs[name])
        if name in _COLUMNS:
            a = a.T
        a = _np.ascontiguousarray(a)
        arrays[f"in_{name}"] = a
        args.append(nc.dram_tensor(f"in_{name}", a.shape, _mybir.dt.from_np(a.dtype), kind="ExternalInput").ap())
    args.append(nc.dram_tensor("out_0", (1, ROWS, TOK, DIM), _mybir.dt.float32, kind="ExternalOutput").ap())
    metaformer_kernel(nc, *args)
    return _run(nc, [arrays], core_ids=[0]).results[0]["out_0"]
```

```python
from contextlib import ExitStack

import concourse.bass as bass
from concourse import mybir

F32 = mybir.dt.float32
F16 = mybir.dt.float16
U32 = mybir.dt.uint32
ALU = mybir.AluOpType
ACT = mybir.ActivationFunctionType
AX = mybir.AxisListType.X

ROWS, TOK, DIM = 16, 128, 64
HEADS, HD = 8, 16
INNER = HEADS * HD
EXPERTS, HID = 8, 128
TOKENS = ROWS * TOK
CHUNK = 4
CHUNKS = ROWS // CHUNK
EPS_OUTER, EPS_LN = 1e-6, 1e-5
CAPACITY = float(-(-TOKENS * 5 // (4 * EXPERTS)))
WSCALE = 64.0
SLOT, STACK = HD, 4 * HD
SHIFT = 3 * HD
QK = HEADS * STACK
K_AT = QK + SLOT
VCOLS = 32
GATED_AT = 4


def metaformer_kernel(nc, x, ln_g, ln_b, Wq, Wkv, Wg, bg, Wo, bo, Wr, br, W1, b1, W2, b2, gamma, beta, out):
    x_d = x.rearrange("a s p d -> p (a s) d")
    out_d = out.rearrange("a s p d -> p (a s) d")
    ctx = ExitStack()
    with ctx:
        def sb(name, shape, dt=F32):
            return ctx.enter_context(nc.sbuf_tensor(name, shape, dt))

        def sem(name):
            return ctx.enter_context(nc.semaphore(name))

        x_all = sb("x_all", [TOK, ROWS, DIM])
        w_in = sb("w_in", [2 * DIM, 4 * INNER])
        w1_in = sb("w1_in", [2 * DIM, EXPERTS, HID])
        w2_in = sb("w2_in", [HID, EXPERTS, DIM])
        wo = sb("wo", [INNER, DIM])
        wr = sb("wr", [DIM, EXPERTS])
        br_row = sb("br_row", [1, EXPERTS])
        b1_t = sb("b1_t", [HID, EXPERTS])
        b2_row = sb("b2_row", [1, EXPERTS, DIM])
        lng_b = sb("lng_b", [TOK, DIM])
        lnb_b = sb("lnb_b", [TOK, DIM])
        bo_b = sb("bo_b", [TOK, DIM])
        bg_b = sb("bg_b", [TOK, INNER])
        gamma_b = sb("gamma_b", [TOK, DIM])
        beta_b = sb("beta_b", [TOK, DIM])
        ident = sb("ident", [128, 128])
        ident16 = sb("ident16", [128, 128], F16)
        ones = sb("ones", [128, 128])
        table_warm = sb("table_warm", [TOK, 1])
        neg_half = sb("neg_half", [TOK, ROWS])
        w_hi = sb("w_hi", [2 * DIM, 4 * INNER], F16)
        w_lo = sb("w_lo", [2 * DIM, 4 * INNER], F16)
        w1_split = sb("w1_split", [2 * DIM, 2, EXPERTS, HID], F16)
        stats = sb("stats", [TOK, ROWS, 6])
        stats2 = sb("stats2", [TOK, ROWS, 6])
        mv = sb("mv", [TOK, ROWS, 2])
        rstd = sb("rstd", [TOK, ROWS])
        xn = sb("xn", [TOK, ROWS, DIM])
        x_bo = sb("x_bo", [TOK, ROWS, DIM])
        x_split = sb("x_split", [TOK, ROWS, 2, DIM], F16)
        x_t = sb("x_t", [2 * DIM, ROWS, TOK], F16)
        qkg = sb("qkg", [TOK, 4, 3 * INNER])
        stack = sb("stack", [TOK, 4, 2 * (K_AT + 2 * SLOT)], F16)
        qk_t = sb("qk_t", [128, 2, 2, 4, TOK], F16)
        q2_t = sb("q2_t", [128, 2, 4, TOK], F16)
        v_aug = sb("v_aug", [TOK, 4, HEADS, VCOLS])
        gate = sb("gate", [TOK, 4, INNER])
        th = sb("th", [TOK, 4, INNER])
        prob = sb("prob", [TOK, 2, 2, 4, TOK])
        u_sb = sb("u_sb", [128, 2, 2, TOK])
        rden = sb("rden", [TOK, 4, HEADS])
        og1 = sb("og1", [TOK, 4, INNER])
        og = sb("og", [TOK, 4, INNER])
        og_t = sb("og_t", [INNER, 2, TOK])
        t_all = sb("t_all", [TOK, ROWS, DIM])
        mv2 = sb("mv2", [TOK, ROWS, 2])
        rstd2 = sb("rstd2", [TOK, ROWS])
        tn = sb("tn", [TOK, ROWS, DIM])
        tn_split = sb("tn_split", [TOK, ROWS, 2, DIM], F16)
        tn_t = sb("tn_t", [2 * DIM, ROWS, TOK], F16)
        t_beta = sb("t_beta", [TOK, ROWS, DIM])
        mean_col = sb("mean_col", [DIM, 1])
        soft = sb("soft", [1, 3, EXPERTS])
        soft_max = sb("soft_max", [1, 3])
        soft_sum = sb("soft_sum", [1, 3])
        soft_inv = sb("soft_inv", [1, 3])
        capped = sb("capped", [1, EXPERTS])
        weights = sb("weights", [1, EXPERTS])
        top_v = sb("top_v", [1, EXPERTS])
        top_i = sb("top_i", [1, EXPERTS], U32)
        mix = sb("mix", [1, 2 + DIM])
        b2_part = sb("b2_part", [1, DIM])
        mix_b = sb("mix_b", [128, 2 + DIM])
        w1_sel = sb("w1_sel", [2 * DIM, 2, 2, HID], F16)
        w2_sel = sb("w2_sel", [HID, 2, DIM])
        b1_sel = sb("b1_sel", [HID, 2])
        hid = sb("hid", [HID, 2, TOKENS])
        tn_b2 = sb("tn_b2", [TOK, ROWS, DIM])
        z = sb("z", [TOK, ROWS, DIM])
        stats3 = sb("stats3", [TOK, ROWS, 6])
        mv3 = sb("mv3", [TOK, ROWS, 2])
        rstd3 = sb("rstd3", [TOK, ROWS])
        zc = sb("zc", [TOK, ROWS, DIM])
        zg = sb("zg", [TOK, ROWS, DIM])
        res = sb("res", [TOK, ROWS, DIM])

        bank = [ctx.enter_context(nc.psum_tensor(f"bank{i}", [128, 512], F32)) for i in range(8)]
        B_PROJ, B_TQK, B_S1, B_S2, B_U, B_UT = 0, 1, 2, 4, 6, 7
        proj_p = bank[B_PROJ][:, :]
        ogt_p = bank[B_PROJ][:, 0:TOK]
        tqk_p = bank[B_TQK][:, :].bitcast(F16).rearrange("c (a p t) -> c a p t", a=2, p=4)
        tq2_p = bank[B_UT][:, 256:512].bitcast(F16).rearrange("c (p t) -> c p t", p=4)
        s1_p = [bank[B_S1 + a][:, :].rearrange("q (p k) -> q p k", p=4) for a in range(2)]
        s2_p = [bank[B_S2 + a][:, :].rearrange("k (p q) -> k p q", p=4) for a in range(2)]
        u_p = bank[B_U][:, 0:2 * TOK].rearrange("c (a q) -> c a q", a=2)
        ut_p = bank[B_UT][:, 0:2 * TOK].rearrange("q (h c) -> q h c", h=HEADS)
        y_p = bank[B_U][:, 2 * TOK:2 * TOK + DIM]
        x_tp_p = bank[B_U][:, 0:256].bitcast(F16).rearrange("c (s t) -> c s t", s=CHUNK)
        tn_tp_p = [bank[B_S1 + c][:, 0:256].bitcast(F16).rearrange("c (s t) -> c s t", s=CHUNK)
                   for c in range(CHUNKS)]
        mean_p = bank[B_TQK][0:DIM, 0:1]
        logits_p = bank[B_PROJ][0:1, 0:EXPERTS]
        mix_p = bank[7][:, 0:2 + DIM]
        z_p = [bank[c][:, 0:CHUNK * DIM].rearrange("t (s d) -> t s d", s=CHUNK) for c in range(CHUNKS)]

        ld = {n: sem(f"loaded_{n}") for n in ("x0", "x1", "x2", "x3", "w", "lng", "lnb", "bo", "bg", "wo",
                                              "w1", "w2", "b1", "b2", "wr", "br", "gamma", "beta")}
        pool_order = sem("pool_order")
        dve_order = sem("dve_order")
        consts = sem("consts")
        ident_ok = sem("ident_ok")
        buffers_ok = sem("buffers_ok")
        w_hi_ok, w_lo_ok = sem("w_hi_ok"), sem("w_lo_ok")
        w1_hi_ok, w1_split_ok = sem("w1_hi_ok"), sem("w1_split_ok")
        mv_ok, rstd_ok, scaled_ok, xn_ok = sem("mv_ok"), sem("rstd_ok"), sem("scaled_ok"), sem("xn_ok")
        x_hi_ok, x_split_ok, x_tp, x_t_ok = sem("x_hi_ok"), sem("x_split_ok"), sem("x_tp"), sem("x_t_ok")
        x_bo_ok = sem("x_bo_ok")
        stats2_ok, mv2_ok, rstd2_ok, tn_ok = sem("stats2_ok"), sem("mv2_ok"), sem("rstd2_ok"), sem("tn_ok")
        tn_hi_ok, tn_split_ok, tn_tp, tn_t_ok = sem("tn_hi_ok"), sem("tn_split_ok"), sem("tn_tp"), sem("tn_t_ok")
        proj_done, qkg_ok, proj_copied = sem("proj_done"), sem("qkg_ok"), sem("proj_copied")
        split_ok, gate_ok, tanh_done = sem("split_ok"), sem("gate_ok"), sem("tanh_done")
        tqk_done, tqk_copied = sem("tqk_done"), sem("tqk_copied")
        s1_done = [sem("s1_even_done"), sem("s1_odd_done")]
        max_done = [sem("max_even_done"), sem("max_odd_done")]
        tq2_done, tq2_copied = sem("tq2_done"), sem("tq2_copied")
        s2_done = [sem("s2_even_done"), sem("s2_odd_done")]
        exp_done = [sem("exp_even_done"), sem("exp_odd_done")]
        pv_done, u_copied, ut_done, ut_read = sem("pv_done"), sem("u_copied"), sem("ut_done"), sem("ut_read")
        og_ok, ogt_done, ogt_copied = sem("og_ok"), sem("ogt_done"), sem("ogt_copied")
        wo_done, t_ok = sem("wo_done"), sem("t_ok")
        mean_done, mean_ok, logits_done = sem("mean_done"), sem("mean_ok"), sem("logits_done")
        r_max, r_exp, mix_ok, mix_done, mix_b_ok = sem("r_max"), sem("r_exp"), sem("mix_ok"), sem("mix_done"), sem("mix_b_ok")
        w1_sel_ok, b1_sel_ok, w2_sel_ok = sem("w1_sel_ok"), sem("b1_sel_ok"), sem("w2_sel_ok")
        fc1_done, gelu_done, fc2_done = sem("fc1_done"), sem("gelu_done"), sem("fc2_done")
        tn_b2_ok, t_beta_ok = sem("tn_b2_ok"), sem("t_beta_ok")
        z_ok, mv3_ok, rstd3_ok, zg_ok, res_ok = sem("z_ok"), sem("mv3_ok"), sem("rstd3_ok"), sem("zg_ok"), sem("res_ok")
        stored = sem("stored")

        block = ctx.enter_context(nc.Block())

        WIDE = [TOK, CHUNK, DIM]

        def pipeline(order, at):
            for t in range(ROWS + max(d for d, _ in order)):
                if t in at:
                    at[t]()
                for distance, stage in order:
                    if 0 <= t - distance < ROWS:
                        stage(t - distance)

        def stack_slots(b, q_slot, k_slot):
            first = q_slot * SLOT
            apart = K_AT + (k_slot - q_slot) * SLOT
            v = stack[:, b, first:first + 2 * apart].rearrange("t (a c) -> t a c", a=2)
            return v[:, :, 0:QK].rearrange("t a (h c) -> t a h c", c=STACK)[:, :, :, 0:SLOT]

        def pair(b, which, p):
            first = which * K_AT + 2 * STACK * p
            return stack[:, b, first:first + 2 * STACK]

        @block.sync
        def _(sp):
            def twice(w):
                return w.unsqueeze(0).broadcast_to([2] + list(w.shape))

            def load_x(c):
                r = slice(c * CHUNK, (c + 1) * CHUNK)
                sp.dma_start(x_all[:, r, :], x_d[:, r, :]).then_inc(ld[f"x{c}"], 16)

            load_x(0)
            for dst, src in ((w_in[:, 0:INNER], Wq), (w_in[:, INNER:2 * INNER], Wkv[:, 0:INNER]),
                             (w_in[:, 2 * INNER:3 * INNER], Wg), (w_in[:, 3 * INNER:4 * INNER], Wkv[:, INNER:2 * INNER])):
                sp.dma_start(dst, twice(src)).then_inc(ld["w"], 16)
            load_x(1)
            load_x(2)
            load_x(3)
            sp.dma_start(wo[:, :], Wo).then_inc(ld["wo"], 16)
            for half in range(2):
                rows = slice(half * DIM, (half + 1) * DIM)
                sp.dma_start(w1_in[rows, :, :], W1.rearrange("e d f -> d e f")).then_inc(ld["w1"], 16)
            sp.dma_start(wr[:, :], Wr).then_inc(ld["wr"], 16)
            sp.dma_start(br_row[0:1, :], br.rearrange("(a e) -> a e", a=1)).then_inc(ld["br"], 16)
            sp.dma_start(w2_in[:, :, :], W2.rearrange("e f d -> f e d")).then_inc(ld["w2"], 16)
            sp.dma_start(b1_t[:, :], b1).then_inc(ld["b1"], 16)
            sp.dma_start(b2_row[0:1, :, :], b2.unsqueeze(0)).then_inc(ld["b2"], 16)
            for c in range(CHUNKS):
                r = slice(c * CHUNK, (c + 1) * CHUNK)
                sp.wait_ge(res_ok, c + 1)
                sp.dma_start(out_d[:, r, :], res[:, r, :]).then_inc(stored, 16)
            sp.wait_ge(stored, 16 * CHUNKS)

        @block.scalar
        def _(act):
            act.wait_ge(consts, 2)
            nc.scalar.activation(table_warm[:, :], neg_half[:, 0:1], ACT.Exp)

            def bcast(v):
                return v.rearrange("(a d) -> a d", a=1).broadcast_to([TOK, v.shape[0]])

            for name, dst, src in (("lng", lng_b, ln_g), ("lnb", lnb_b, ln_b), ("bg", bg_b, bg), ("bo", bo_b, bo),
                                   ("gamma", gamma_b, gamma), ("beta", beta_b, beta)):
                act.dma_start(dst[:, :], bcast(src)).then_inc(ld[name], 16)

            def high_x(c):
                r = slice(c * CHUNK, (c + 1) * CHUNK)
                act.wait_ge(xn_ok, c + 1)
                nc.scalar.activation(x_split[:, r, 0, :], xn[:, r, :], ACT.Copy).then_inc(x_hi_ok, 1)

            def copy_x_t(c):
                act.wait_ge(x_tp, c + 1)
                nc.scalar.activation(x_t[:, c * CHUNK:(c + 1) * CHUNK, :], x_tp_p, ACT.Copy).then_inc(x_t_ok, 1)

            def projections(s):
                b = s % 4
                act.wait_ge(proj_done, s + 1)
                if s >= 4:
                    act.wait_ge(split_ok, s - 3)
                    act.wait_ge(gate_ok, s - 3)
                    act.wait_ge(tq2_done, s - 3)
                qk = proj_p[:, 0:2 * INNER].rearrange("t (a h c) -> t a h c", a=2, h=HEADS)
                nc.scalar.activation(stack_slots(b, 0, 0), qk, ACT.Copy, scale=1 / WSCALE)
                nc.scalar.activation(qkg[:, b, :], proj_p[:, 0:3 * INNER], ACT.Copy,
                                     scale=1 / WSCALE).then_inc(qkg_ok, 1)
                nc.scalar.activation(stack_slots(b, 1, 2), qk, ACT.Copy, scale=1 / WSCALE)
                if s >= 4:
                    act.wait_ge(pv_done, s - 3)
                nc.scalar.activation(v_aug[:, b, :, 0:HD],
                                     proj_p[:, 3 * INNER:4 * INNER].rearrange("t (h c) -> t h c", h=HEADS),
                                     ACT.Copy, scale=1 / WSCALE).then_inc(proj_copied, 1)

            def gates(s):
                b = s % 4
                act.wait_ge(gate_ok, s + 1)
                if s >= 4:
                    act.wait_ge(ut_read, s - 3)
                nc.scalar.activation(th[:, b, :], gate[:, b, :], ACT.Tanh, scale=0.5).then_inc(tanh_done, 1)

            def probabilities(s):
                b = s % 2
                for a in range(2):
                    act.wait_ge(s2_done[a], s + 1)
                    if s >= 2:
                        act.wait_ge(pv_done, s - 1)
                    nc.scalar.activation(prob[:, b, a], s2_p[a], ACT.Exp, scale=HD ** -0.5).then_inc(exp_done[a], 1)

            def outputs(s):
                b = s % 2
                act.wait_ge(pv_done, s + 1)
                if s >= 2:
                    act.wait_ge(ut_done, s - 1)
                nc.scalar.activation(u_sb[:, b], u_p, ACT.Copy).then_inc(u_copied, 1)

            def gated(s):
                b = s % 2
                act.wait_ge(ogt_done, s + 1)
                if s >= 2:
                    act.wait_ge(wo_done, s - 1)
                nc.scalar.activation(og_t[:, b, :], ogt_p, ACT.Copy).then_inc(ogt_copied, 1)

            def high_w1():
                act.wait_ge(ld["w1"], 32)
                for e in range(0, EXPERTS, 4):
                    nc.scalar.activation(w1_split[:, 0, e:e + 4], w1_in[:, e:e + 4, :], ACT.Copy,
                                         scale=WSCALE).then_inc(w1_hi_ok, 1)

            def high_t(c):
                r = slice(c * CHUNK, (c + 1) * CHUNK)
                act.wait_ge(tn_ok, c + 1)
                nc.scalar.activation(tn_split[:, r, 0, :], tn[:, r, :], ACT.Copy).then_inc(tn_hi_ok, 1)

            def copy_tn_t(c):
                act.wait_ge(tn_tp, c + 1)
                nc.scalar.activation(tn_t[:, c * CHUNK:(c + 1) * CHUNK, :], tn_tp_p[c], ACT.Copy).then_inc(tn_t_ok, 1)

            act.wait_ge(ld["w"], 4 * 16)
            nc.scalar.activation(w_hi[:, :], w_in[:, :], ACT.Copy, scale=WSCALE).then_inc(w_hi_ok, 1)
            high_x(0)
            copy_x_t(0)
            pipeline([(0, projections), (3, outputs), (4, gated), (2, probabilities), (1, gates)],
                     {1: lambda: high_x(1), 2: lambda: (copy_x_t(1), high_x(2)), 3: lambda: (copy_x_t(2), high_x(3)),
                      4: lambda: copy_x_t(3), 6: high_w1, 13: lambda: high_t(0), 17: lambda: high_t(1),
                      19: lambda: (copy_tn_t(0), copy_tn_t(1))})
            high_t(2)
            copy_tn_t(2)

            def exponentials(n, src, width):
                act.wait_ge(r_max, n + 1)
                nc.scalar.activation(soft[0:1, n, 0:width], src, ACT.Exp, bias=soft_max[0:1, n:n + 1],
                                     accum_out=soft_sum[0:1, n:n + 1]).then_inc(r_exp, 1)

            high_t(3)
            exponentials(0, logits_p, EXPERTS)
            copy_tn_t(3)
            exponentials(1, capped[0:1, :], EXPERTS)
            exponentials(2, top_v[0:1, 0:2], 2)
            nc.scalar.activation(table_warm[:, :], neg_half[:, 0:1], ACT.Gelu)
            act.wait_ge(b1_sel_ok, 1)
            for c in range(CHUNKS):
                for j in range(2):
                    n = 2 * c + j
                    act.wait_ge(fc1_done, n + 1)
                    nc.scalar.activation(hid[:, j, c * 512:(c + 1) * 512], bank[n][:, :], ACT.Gelu,
                                         bias=b1_sel[:, j:j + 1], scale=1 / WSCALE).then_inc(gelu_done, 1)

        @block.vector
        def _(dve):
            order = [0]

            def then_next(instruction):
                order[0] += 1
                instruction.then_inc(dve_order, 1)
                dve.wait_ge(dve_order, order[0])

            nc.vector.memset(ones[:, :], 1.0).then_inc(consts, 1)
            nc.vector.memset(neg_half[:, :], -0.5).then_inc(consts, 1)

            def moments(c, src, stats, mv_, mv_sem):
                rows = range(c * CHUNK, (c + 1) * CHUNK)
                for s in rows:
                    last = nc.vector.bn_stats(stats[:, s, :], src[:, s, :])
                then_next(last)
                for s in rows:
                    last = nc.vector.bn_aggr(mv_[:, s, :], stats[:, s, :])
                last.then_inc(mv_sem, 1)

            def centered(c, src, mv_, mv_sem, dst):
                r = slice(c * CHUNK, (c + 1) * CHUNK)
                dve.wait_ge(mv_sem, c + 1)
                then_next(nc.vector.tensor_tensor(dst[:, r, :], src[:, r, :], mv_[:, r, 0:1].broadcast_to(WIDE), ALU.subtract))

            def scaled(c, rstd_, rstd_sem, dst):
                r = slice(c * CHUNK, (c + 1) * CHUNK)
                dve.wait_ge(rstd_sem, c + 1)
                return nc.vector.tensor_tensor(dst[:, r, :], dst[:, r, :], rstd_[:, r].unsqueeze(2).broadcast_to(WIDE), ALU.mult)

            def norm_x(c):
                centered(c, x_all, mv, mv_ok, xn)
                scaled(c, rstd, rstd_ok, xn).then_inc(scaled_ok, 1)

            def low_x(c):
                r = slice(c * CHUNK, (c + 1) * CHUNK)
                dve.wait_ge(x_hi_ok, c + 1)
                nc.vector.tensor_tensor(x_split[:, r, 1, :], xn[:, r, :], x_split[:, r, 0, :], ALU.subtract).then_inc(x_split_ok, 1)

            def low(s):
                b = s % 4
                dve.wait_ge(qkg_ok, s + 1)
                nc.vector.tensor_tensor(stack_slots(b, 2, 1),
                                        qkg[:, b, 0:2 * INNER].rearrange("t (a h c) -> t a h c", a=2, h=HEADS),
                                        stack_slots(b, 0, 0), ALU.subtract).then_inc(split_ok, 1)

            def copy_stacks(s):
                b = s % 2
                dve.wait_ge(tqk_done, s + 1)
                if s >= 2:
                    for a in range(2):
                        dve.wait_ge(s2_done[a], s - 1)
                nc.vector.tensor_copy(qk_t[:, b], tqk_p).then_inc(tqk_copied, 1)

            def maxima(s):
                b = s % 4
                for a in range(2):
                    dve.wait_ge(s1_done[a], s + 1)
                    q = stack[:, b, 0:QK].rearrange("t (p a c) -> t p a c", p=4, a=2)
                    nc.vector.tensor_reduce(q[:, :, a, SHIFT], s1_p[a], AX, ALU.max, negate=True).then_inc(max_done[a], 1)

            def copy_q(s):
                b = s % 2
                dve.wait_ge(tq2_done, s + 1)
                if s >= 2:
                    for a in range(2):
                        dve.wait_ge(s2_done[a], s - 1)
                nc.vector.tensor_copy(q2_t[:, b], tq2_p).then_inc(tq2_copied, 1)

            def gate_outputs(s):
                b = s % 4
                dve.wait_ge(ut_done, s + 1)
                dve.wait_ge(tanh_done, s + 1)
                if s >= 4:
                    dve.wait_ge(og_ok, s - 3)
                nc.vector.reciprocal(rden[:, b, :], ut_p[:, :, HD])
                nc.vector.scalar_tensor_tensor(out=og1[:, b, :].rearrange("t (h c) -> t h c", h=HEADS),
                                               in0=th[:, b, :].rearrange("t (h c) -> t h c", h=HEADS), scalar=1.0,
                                               in1=ut_p[:, :, 0:HD], op0=ALU.add, op1=ALU.mult).then_inc(ut_read, 1)

            def residual(s):
                dve.wait_ge(wo_done, s + 1)
                dve.wait_ge(x_bo_ok, s // CHUNK + 1)
                nc.vector.tensor_tensor(t_all[:, s, :], y_p, x_bo[:, s, :], ALU.add).then_inc(t_ok, 1)

            def row_stats(s):
                dve.wait_ge(t_ok, s + 1)
                nc.vector.bn_stats(stats2[:, s, :], t_all[:, s, :]).then_inc(stats2_ok, 1)

            def row_moments(s):
                dve.wait_ge(stats2_ok, s + 1)
                nc.vector.bn_aggr(mv2[:, s, :], stats2[:, s, :]).then_inc(mv2_ok, 1)

            def norm_t(c):
                r = slice(c * CHUNK, (c + 1) * CHUNK)
                dve.wait_ge(mv2_ok, (c + 1) * CHUNK)
                then_next(nc.vector.tensor_tensor(tn[:, r, :], t_all[:, r, :], mv2[:, r, 0:1].broadcast_to(WIDE), ALU.subtract))
                scaled(c, rstd2, rstd2_ok, tn).then_inc(tn_ok, 1)

            def low_w1():
                for e in range(0, EXPERTS, 4):
                    dve.wait_ge(w1_hi_ok, e // 4 + 1)
                    nc.vector.scalar_tensor_tensor(out=w1_split[:, 1, e:e + 4], in0=w1_in[:, e:e + 4, :], scalar=WSCALE,
                                                   in1=w1_split[:, 0, e:e + 4], op0=ALU.mult,
                                                   op1=ALU.subtract).then_inc(w1_split_ok, 1)

            dve.wait_ge(ld["x0"], 16)
            moments(0, x_all, stats, mv, mv_ok)
            centered(0, x_all, mv, mv_ok, xn)
            then_next(scaled(0, rstd, rstd_ok, xn))
            first = xn[:, 0:CHUNK, :]
            dve.wait_ge(ld["lng"], 16)
            then_next(nc.vector.tensor_tensor(first, first, lng_b[:, :].unsqueeze(1).broadcast_to(WIDE), ALU.mult))
            dve.wait_ge(ld["lnb"], 16)
            nc.vector.tensor_tensor(first, first, lnb_b[:, :].unsqueeze(1).broadcast_to(WIDE), ALU.add).then_inc(xn_ok, 1)
            dve.wait_ge(w_hi_ok, 1)
            nc.vector.scalar_tensor_tensor(out=w_lo[:, :], in0=w_in[:, :], scalar=WSCALE, in1=w_hi[:, :],
                                           op0=ALU.mult, op1=ALU.subtract).then_inc(w_lo_ok, 1)
            low_x(0)
            for c in range(1, CHUNKS):
                dve.wait_ge(ld[f"x{c}"], 16)
                moments(c, x_all, stats, mv, mv_ok)
            norm_x(1)
            dve.wait_ge(buffers_ok, 1)

            pipeline([(0, low), (1, maxima), (3, gate_outputs), (5, residual), (6, row_stats), (7, row_moments),
                      (0, copy_stacks), (1, copy_q)],
                     {1: lambda: (low_x(1), norm_x(2)), 2: lambda: (low_x(2), norm_x(3)), 3: lambda: low_x(3),
                      7: low_w1, 12: lambda: norm_t(0), 16: lambda: norm_t(1), 20: lambda: norm_t(2)})
            norm_t(3)

            dve.wait_ge(mean_done, 1)
            nc.vector.tensor_scalar(mean_col[:, :], mean_p, 1.0 / TOKENS, None, ALU.mult).then_inc(mean_ok, 1)
            dve.wait_ge(logits_done, 1)
            nc.vector.tensor_reduce(soft_max[0:1, 0:1], logits_p, AX, ALU.max, negate=True).then_inc(r_max, 1)
            dve.wait_ge(r_exp, 1)
            then_next(nc.vector.reciprocal(soft_inv[0:1, 0:1], soft_sum[0:1, 0:1]))
            then_next(nc.vector.tensor_scalar(capped[0:1, :], soft[0:1, 0, :], soft_inv[0:1, 0:1], CAPACITY / TOKENS,
                                              ALU.mult, ALU.min))
            nc.vector.tensor_reduce(soft_max[0:1, 1:2], capped[0:1, :], AX, ALU.max, negate=True).then_inc(r_max, 1)
            dve.wait_ge(r_exp, 2)
            then_next(nc.vector.reciprocal(soft_inv[0:1, 1:2], soft_sum[0:1, 1:2]))
            then_next(nc.vector.tensor_scalar(weights[0:1, :], soft[0:1, 1, :], soft_inv[0:1, 1:2], None, ALU.mult))
            then_next(nc.vector.max(top_v[0:1, :], weights[0:1, :]))
            then_next(nc.vector.max_index(top_i[0:1, :], top_v[0:1, :], weights[0:1, :]))
            nc.vector.tensor_scalar(soft_max[0:1, 2:3], top_v[0:1, 0:1], -1.0, None, ALU.mult).then_inc(r_max, 1)
            expert = [dve.value_load(top_i[0:1, j:j + 1], min_val=0, max_val=EXPERTS - 1) for j in range(2)]
            dve.wait_ge(w1_split_ok, 2)
            for j in range(2):
                nc.vector.tensor_copy(w1_sel[:, j], w1_split[:, :, bass.ds(expert[j], 1), :].rearrange(
                    "c l e f -> c l (e f)")).then_inc(w1_sel_ok, 1)
            dve.wait_ge(ld["b1"], 16)
            for j in range(2):
                last = nc.vector.tensor_copy(b1_sel[:, j:j + 1], b1_t[:, bass.ds(expert[j], 1)])
            last.then_inc(b1_sel_ok, 1)
            dve.wait_ge(r_exp, 3)
            then_next(nc.vector.reciprocal(soft_inv[0:1, 2:3], soft_sum[0:1, 2:3]))
            then_next(nc.vector.tensor_scalar(mix[0:1, 0:2], soft[0:1, 2, 0:2], soft_inv[0:1, 2:3], None, ALU.mult))
            dve.wait_ge(ld["b2"], 16)
            then_next(nc.vector.tensor_scalar(b2_part[0:1, :], b2_row[0:1, bass.ds(expert[0], 1), :].rearrange(
                "a e d -> a (e d)"), mix[0:1, 0:1], None, ALU.mult))
            nc.vector.scalar_tensor_tensor(out=mix[0:1, 2:2 + DIM], in0=b2_row[0:1, bass.ds(expert[1], 1), :].rearrange(
                "a e d -> a (e d)"), scalar=mix[0:1, 1:2], in1=b2_part[0:1, :], op0=ALU.mult, op1=ALU.add).then_inc(mix_ok, 1)
            dve.wait_ge(mix_done, 1)
            nc.vector.tensor_copy(mix_b[:, :], mix_p).then_inc(mix_b_ok, 1)
            dve.wait_ge(mix_b_ok, 1)
            dve.wait_ge(ld["w2"], 16)
            for j in range(2):
                nc.vector.tensor_scalar(w2_sel[:, j, :], w2_in[:, bass.ds(expert[j], 1), :].rearrange("f e d -> f (e d)"),
                                        mix_b[:, j:j + 1], None, ALU.mult).then_inc(w2_sel_ok, 1)

            def norm_z(c):
                r = slice(c * CHUNK, (c + 1) * CHUNK)
                dve.wait_ge(fc2_done, c + 1)
                dve.wait_ge(tn_b2_ok, c + 1)
                then_next(nc.vector.tensor_tensor(z[:, r, :], z_p[c], tn_b2[:, r, :], ALU.add))
                moments(c, z, stats3, mv3, mv3_ok)
                centered(c, z, mv3, mv3_ok, zc)
                dve.wait_ge(ld["gamma"], 16)
                nc.vector.tensor_tensor(zg[:, r, :], zc[:, r, :], gamma_b[:, :].unsqueeze(1).broadcast_to(WIDE),
                                        ALU.mult).then_inc(zg_ok, 1)

            def result(c):
                dve.wait_ge(rstd3_ok, c + 1)
                dve.wait_ge(zg_ok, c + 1)
                dve.wait_ge(t_beta_ok, c + 1)
                for s in range(c * CHUNK, (c + 1) * CHUNK):
                    last = nc.vector.scalar_tensor_tensor(out=res[:, s, :], in0=zg[:, s, :], scalar=rstd3[:, s:s + 1],
                                                          in1=t_beta[:, s, :], op0=ALU.mult, op1=ALU.add)
                last.then_inc(res_ok, 1)

            for c in range(CHUNKS):
                norm_z(c)
                if c > 0:
                    result(c - 1)
            result(CHUNKS - 1)

        @block.gpsimd
        def _(pool):
            order = [0]

            def then_next(instruction):
                order[0] += 1
                instruction.then_inc(pool_order, 1)
                pool.wait_ge(pool_order, order[0])

            def power(c, mv_, rstd_, scale, eps, rstd_sem):
                r = slice(c * CHUNK, (c + 1) * CHUNK)
                then_next(nc.gpsimd.tensor_scalar(rstd_[:, r], mv_[:, r, 1], scale, eps, ALU.mult, ALU.add))
                nc.gpsimd.tensor_tensor(rstd_[:, r], rstd_[:, r], neg_half[:, r], ALU.pow).then_inc(rstd_sem, 1)

            def power_x(c):
                pool.wait_ge(mv_ok, c + 1)
                power(c, mv, rstd, 1.0 + EPS_LN, EPS_LN * EPS_OUTER, rstd_ok)

            def weight_x(c):
                r = slice(c * CHUNK, (c + 1) * CHUNK)
                pool.wait_ge(scaled_ok, c)
                pool.wait_ge(ld["lng"], 16)
                then_next(nc.gpsimd.tensor_tensor(xn[:, r, :], xn[:, r, :], lng_b[:, :].unsqueeze(1).broadcast_to(WIDE), ALU.mult))
                pool.wait_ge(ld["lnb"], 16)
                nc.gpsimd.tensor_tensor(xn[:, r, :], xn[:, r, :], lnb_b[:, :].unsqueeze(1).broadcast_to(WIDE),
                                        ALU.add).then_inc(xn_ok, 1)

            def add_bo(c):
                r = slice(c * CHUNK, (c + 1) * CHUNK)
                pool.wait_ge(ld[f"x{c}"], 16)
                pool.wait_ge(ld["bo"], 16)
                nc.gpsimd.tensor_tensor(x_bo[:, r, :], x_all[:, r, :], bo_b[:, :].unsqueeze(1).broadcast_to(WIDE),
                                        ALU.add).then_inc(x_bo_ok, 1)

            def power_t(c):
                pool.wait_ge(mv2_ok, (c + 1) * CHUNK)
                power(c, mv2, rstd2, 1.0, EPS_LN, rstd2_ok)

            def low_t(c):
                r = slice(c * CHUNK, (c + 1) * CHUNK)
                pool.wait_ge(tn_ok, c + 1)
                pool.wait_ge(tn_hi_ok, c + 1)
                nc.gpsimd.tensor_tensor(tn_split[:, r, 1, :], tn[:, r, :], tn_split[:, r, 0, :], ALU.subtract).then_inc(tn_split_ok, 1)

            def add_beta(c):
                r = slice(c * CHUNK, (c + 1) * CHUNK)
                pool.wait_ge(ld["beta"], 16)
                pool.wait_ge(t_ok, (c + 1) * CHUNK)
                nc.gpsimd.tensor_tensor(t_beta[:, r, :], t_all[:, r, :], beta_b[:, :].unsqueeze(1).broadcast_to(WIDE),
                                        ALU.add).then_inc(t_beta_ok, 1)

            def gate_input(s):
                b = s % 4
                pool.wait_ge(qkg_ok, s + 1)
                if s >= 4:
                    pool.wait_ge(tanh_done, s - 3)
                nc.gpsimd.tensor_tensor(gate[:, b, :], qkg[:, b, 2 * INNER:3 * INNER], bg_b[:, :], ALU.add).then_inc(gate_ok, 1)

            def divide(s):
                b = s % 4
                pool.wait_ge(ut_read, s + 1)
                if s >= 4:
                    pool.wait_ge(ogt_done, s - 3)
                nc.gpsimd.tensor_tensor(og[:, b, :].rearrange("t (h c) -> t h c", h=HEADS),
                                        og1[:, b, :].rearrange("t (h c) -> t h c", h=HEADS),
                                        rden[:, b, :].unsqueeze(2).broadcast_to([TOK, HEADS, HD]),
                                        ALU.mult).then_inc(og_ok, 1)

            pool.wait_ge(consts, 2)
            nc.gpsimd.affine_select(out=ident[:, :], in_=ones[:, :], compare_op=ALU.is_equal, fill=0.0, base=0,
                                    pattern=[[-1, 128]], channel_multiplier=1).then_inc(ident_ok, 1)
            pool.wait_ge(ident_ok, 1)
            nc.gpsimd.tensor_copy(ident16[:, :], ident[:, :]).then_inc(ident_ok, 1)
            power_x(0)
            for first in (0, K_AT):
                v = stack[:, :, first:first + QK].rearrange("t b (h c) -> t b h c", c=STACK)
                nc.gpsimd.memset(v[:, :, :, SHIFT:STACK], 0.0)
            then_next(nc.gpsimd.memset(v_aug[:, :, :, HD:VCOLS], 0.0))
            nc.gpsimd.memset(v[:, :, :, SHIFT], 1.0)
            then_next(nc.gpsimd.memset(v_aug[:, :, :, HD], 2.0))
            pool.sem_inc(buffers_ok, 1)
            for c in range(1, CHUNKS):
                power_x(c)
            pool.wait_ge(ld["bg"], 16)
            pipeline([(0, gate_input), (3, divide)],
                     {1: lambda: weight_x(1), 2: lambda: weight_x(2), 3: lambda: weight_x(3),
                      4: lambda: add_bo(0), 5: lambda: add_bo(1), 6: lambda: add_bo(2), 7: lambda: add_bo(3),
                      11: lambda: power_t(0), 13: lambda: low_t(0), 15: lambda: power_t(1), 17: lambda: low_t(1)})
            add_beta(0)
            power_t(2)
            low_t(2)
            add_beta(1)
            power_t(3)
            add_beta(2)
            low_t(3)
            add_beta(3)
            pool.wait_ge(mix_b_ok, 1)
            for c in range(CHUNKS):
                r = slice(c * CHUNK, (c + 1) * CHUNK)
                if c > 1:
                    pool.wait_ge(mv3_ok, c - 1)
                    power(c - 2, mv3, rstd3, 1.0, EPS_LN, rstd3_ok)
                nc.gpsimd.tensor_tensor(tn_b2[:, r, :], tn[:, r, :], mix_b[:, 2:2 + DIM].unsqueeze(1).broadcast_to(WIDE),
                                        ALU.add).then_inc(tn_b2_ok, 1)
            for c in range(2, CHUNKS):
                pool.wait_ge(mv3_ok, c + 1)
                power(c, mv3, rstd3, 1.0, EPS_LN, rstd3_ok)

        @block.tensor
        def _(pe):
            def transpose_x(c):
                pe.wait_ge(x_split_ok, c + 1)
                if c > 0:
                    pe.wait_ge(x_t_ok, c)
                if c == 3:
                    pe.wait_ge(u_copied, 1)
                for i in range(CHUNK):
                    last = nc.tensor.transpose(x_tp_p[:, i, :], x_split[:, c * CHUNK + i].rearrange("t l d -> t (l d)"),
                                               ident16[:, :])
                last.then_inc(x_tp, 1)

            def project(s):
                pe.wait_ge(x_t_ok, s // CHUNK + 1)
                if s > 0:
                    pe.wait_ge(proj_copied, s)
                if s > GATED_AT:
                    pe.wait_ge(ogt_copied, s - GATED_AT)
                nc.tensor.matmul(proj_p, x_t[:, s, :], w_hi[:, :], start=True, stop=False)
                nc.tensor.matmul(proj_p, x_t[:, s, :], w_lo[:, :], start=False, stop=True).then_inc(proj_done, 1)

            def transpose_stacks(s):
                b = s % 4
                pe.wait_ge(split_ok, s + 1)
                pe.wait_ge(proj_copied, s + 1)
                if s > 0:
                    pe.wait_ge(tqk_copied, s)
                for which in range(2):
                    for p in range(4):
                        last = nc.tensor.transpose(tqk_p[:, which, p, :], pair(b, which, p), ident16[:, :])
                last.then_inc(tqk_done, 1)

            def scores(a):
                def stage(s):
                    b, r = s % 2, slice(64 * a, 64 * a + SHIFT)
                    pe.wait_ge(tqk_copied, s + 1)
                    if s > 0:
                        pe.wait_ge(max_done[a], s)
                    for p in range(4):
                        last = nc.tensor.matmul(s1_p[a][:, p, :], qk_t[r, b, 0, p, :], qk_t[r, b, 1, p, :],
                                                start=True, stop=True)
                    last.then_inc(s1_done[a], 1)
                return stage

            def transpose_q(s):
                b = s % 4
                for a in range(2):
                    pe.wait_ge(max_done[a], s + 1)
                if s > 0:
                    pe.wait_ge(tq2_copied, s)
                if s > 1:
                    pe.wait_ge(ut_read, s - 1)
                for p in range(4):
                    last = nc.tensor.transpose(tq2_p[:, p, :], pair(b, 0, p), ident16[:, :])
                last.then_inc(tq2_done, 1)

            def shifted_scores(a):
                def stage(s):
                    b, r = s % 2, slice(64 * a, 64 * a + STACK)
                    pe.wait_ge(tq2_copied, s + 1)
                    if s > 0:
                        pe.wait_ge(exp_done[a], s)
                    for p in range(4):
                        last = nc.tensor.matmul(s2_p[a][:, p, :], qk_t[r, b, 1, p, :], q2_t[r, b, p, :],
                                                start=True, stop=True)
                    last.then_inc(s2_done[a], 1)
                return stage

            def values(s):
                b = s % 4
                for a in range(2):
                    pe.wait_ge(exp_done[a], s + 1)
                pe.wait_ge(proj_copied, s + 1)
                pe.wait_ge(x_t_ok, CHUNKS if s > 0 else CHUNKS - 1)
                if s > 0:
                    pe.wait_ge(u_copied, s)
                if s > 2:
                    pe.wait_ge(t_ok, s - 2)
                for a in range(2):
                    for p in range(4):
                        last = nc.tensor.matmul(u_p[32 * p:32 * p + 32, a, :], v_aug[:, b, 2 * p + a, :],
                                                prob[:, s % 2, a, p, :], start=True, stop=True)
                last.then_inc(pv_done, 1)

            def transpose_outputs(s):
                pe.wait_ge(u_copied, s + 1)
                pe.wait_ge(tq2_copied, min(s + 2, ROWS))
                if s == ROWS - 1:
                    pe.wait_ge(ut_read, s)
                for a in range(2):
                    last = nc.tensor.transpose(ut_p.rearrange("q (p a) c -> q p a c", a=2)[:, :, a, :],
                                               u_sb[:, s % 2, a, :], ident[:, :])
                last.then_inc(ut_done, 1)

            def transpose_gated(s):
                pe.wait_ge(og_ok, s + 1)
                pe.wait_ge(proj_copied, min(s + GATED_AT + 1, ROWS))
                if s > 0:
                    pe.wait_ge(ogt_copied, s)
                nc.tensor.transpose(ogt_p, og[:, s % 4, :], ident[:, :]).then_inc(ogt_done, 1)

            def project_out(s):
                pe.wait_ge(ogt_copied, s + 1)
                pe.wait_ge(u_copied, min(s + 3, ROWS))
                if s > 0:
                    pe.wait_ge(t_ok, s)
                nc.tensor.matmul(y_p, og_t[:, s % 2, :], wo[:, :], start=True, stop=True).then_inc(wo_done, 1)

            def sum_tokens(c):
                pe.wait_ge(tn_ok, c + 1)
                if c == 0:
                    pe.wait_ge(tqk_copied, ROWS)
                for s in range(c * CHUNK, (c + 1) * CHUNK):
                    last = nc.tensor.matmul(mean_p, tn[:, s, :], ones[:, 0:1], start=s == 0, stop=s == ROWS - 1)
                if c == CHUNKS - 1:
                    last.then_inc(mean_done, 1)

            def transpose_tn(c):
                pe.wait_ge(tn_split_ok, c + 1)
                if c < 2:
                    pe.wait_ge(max_done[c], ROWS)
                else:
                    pe.wait_ge(exp_done[c - 2], ROWS)
                for i in range(CHUNK):
                    last = nc.tensor.transpose(tn_tp_p[c][:, i, :],
                                               tn_split[:, c * CHUNK + i].rearrange("t l d -> t (l d)"), ident16[:, :])
                last.then_inc(tn_tp, 1)

            pe.wait_ge(ident_ok, 2)
            transpose_x(0)
            pe.wait_ge(w_hi_ok, 1)
            pe.wait_ge(w_lo_ok, 1)
            pe.wait_ge(ld["wo"], 16)

            def stacks_ready():
                pe.wait_ge(buffers_ok, 1)

            pipeline([(0, project), (1, transpose_stacks), (2, transpose_q), (3, values), (1, scores(0)),
                      (GATED_AT, transpose_gated), (1, scores(1)), (2, shifted_scores(0)), (2, shifted_scores(1)),
                      (3, transpose_outputs), (5, project_out)],
                     {1: stacks_ready, 2: lambda: transpose_x(1), 3: lambda: transpose_x(2), 4: lambda: transpose_x(3),
                      18: lambda: (sum_tokens(0), sum_tokens(1)), 19: lambda: (transpose_tn(0), transpose_tn(1))})
            sum_tokens(2)
            transpose_tn(2)
            pe.wait_ge(ld["wr"], 16)
            pe.wait_ge(ld["br"], 16)
            nc.tensor.matmul(logits_p, ones[0:1, 0:1], br_row[0:1, :], start=True, stop=False)
            sum_tokens(3)
            pe.wait_ge(mean_ok, 1)
            nc.tensor.matmul(logits_p, mean_col[:, :], wr[:, :], start=False, stop=True).then_inc(logits_done, 1)
            transpose_tn(3)

            def fc1(c):
                pe.wait_ge(tn_t_ok, c + 1)
                for j in range(2):
                    n = 2 * c + j
                    if c == 0:
                        pe.wait_ge(w1_sel_ok, j + 1)
                    if n in (2, 4):
                        pe.wait_ge(tn_t_ok, n // 2 + 2)
                    if n == 7:
                        pe.wait_ge(mix_b_ok, 1)
                    for part in range(2):
                        last = nc.tensor.matmul(bank[n][:, :], w1_sel[:, j, part, :],
                                                tn_t[:, c * CHUNK:(c + 1) * CHUNK, :].rearrange("c s t -> c (s t)"),
                                                start=part == 0, stop=part == 1)
                    last.then_inc(fc1_done, 1)

            def fc2(c):
                pe.wait_ge(gelu_done, 2 * c + 2)
                pe.wait_ge(w2_sel_ok, 2)
                for i in range(CHUNK):
                    s = c * CHUNK + i
                    for j in range(2):
                        last = nc.tensor.matmul(z_p[c][:, i, :], hid[:, j, s * TOK:(s + 1) * TOK], w2_sel[:, j, :],
                                                start=j == 0, stop=j == 1)
                last.then_inc(fc2_done, 1)

            fc1(0)
            pe.wait_ge(mix_ok, 1)
            nc.tensor.matmul(mix_p, ones[0:1, :], mix[0:1, :], start=True, stop=True).then_inc(mix_done, 1)
            fc1(1)
            for c in range(CHUNKS):
                fc2(c)
                if c + 2 < CHUNKS:
                    fc1(c + 2)


_ORDER = ["x", "L0_conv_ln_g", "L0_conv_ln_b", "L0_conv_Wq", "L0_conv_Wkv", "L0_conv_Wg", "L0_conv_bg", "L0_conv_Wo",
          "L0_conv_bo", "L0_ffn_Wr", "L0_ffn_br", "L0_ffn_W1", "L0_ffn_b1", "L0_ffn_W2", "L0_ffn_b2", "L0_ffn_gamma",
          "L0_ffn_beta"]

_COLUMNS = ("L0_ffn_b1",)


def kernel(**inputs):
    import numpy as _np
    import concourse.bacc as _bacc
    from concourse import mybir as _mybir
    from concourse.bass_utils import run_bass_kernel_spmd as _run

    nc = _bacc.Bacc("TRN2", target_bir_lowering=False, num_devices=1)
    arrays, args = {}, []
    for name in _ORDER:
        a = _np.asarray(inputs[name])
        if name in _COLUMNS:
            a = a.T
        a = _np.ascontiguousarray(a)
        arrays[f"in_{name}"] = a
        args.append(nc.dram_tensor(f"in_{name}", a.shape, _mybir.dt.from_np(a.dtype), kind="ExternalInput").ap())
    args.append(nc.dram_tensor("out_0", (1, ROWS, TOK, DIM), _mybir.dt.float32, kind="ExternalOutput").ap())
    metaformer_kernel(nc, *args)
    return _run(nc, [arrays], core_ids=[0]).results[0]["out_0"]
```

```python
from contextlib import ExitStack

import concourse.bass as bass
from concourse import mybir

F32 = mybir.dt.float32
F16 = mybir.dt.float16
U32 = mybir.dt.uint32
ALU = mybir.AluOpType
ACT = mybir.ActivationFunctionType
AX = mybir.AxisListType.X

ROWS, TOK, DIM = 16, 128, 64
HEADS, HD = 8, 16
INNER = HEADS * HD
EXPERTS, HID = 8, 128
TOKENS = ROWS * TOK
CHUNK = 4
CHUNKS = ROWS // CHUNK
EPS_OUTER, EPS_LN = 1e-6, 1e-5
CAPACITY = float(-(-TOKENS * 5 // (4 * EXPERTS)))
WSCALE = 64.0
SLOT, STACK = HD, 4 * HD
SHIFT = 3 * HD
QK = HEADS * STACK
K_AT = QK + SLOT
VCOLS = 32
STEPS = ROWS + 8
GATED_LATE = 4
NORM_AT, WEIGHT_AT, SPLIT_AT, TRANSPOSE_AT = (0, 0, 1, 2), (0, 1, 2, 3), (0, 2, 3, 4), (0, 3, 4, 5)
W1_HIGH_AT, W1_LOW_AT = 2, 3
WARM_START, WARM_NORM, WARM_ROUTING = 7, 1, 5


def metaformer_kernel(nc, x, ln_g, ln_b, Wq, Wkv, Wg, bg, Wo, bo, Wr, br, W1, b1, W2, b2, gamma, beta, out):
    x_d = x.rearrange("a s p d -> p (a s) d")
    out_d = out.rearrange("a s p d -> p (a s) d")
    ctx = ExitStack()
    with ctx:
        def sb(name, shape, dt=F32):
            return ctx.enter_context(nc.sbuf_tensor(name, shape, dt))

        def sem(name):
            return ctx.enter_context(nc.semaphore(name))

        x_all = sb("x_all", [TOK, ROWS, DIM])
        w_in = sb("w_in", [2 * DIM, 4 * INNER])
        w1_in = sb("w1_in", [2 * DIM, EXPERTS, HID])
        w2_in = sb("w2_in", [HID, EXPERTS, DIM])
        wo = sb("wo", [INNER, DIM])
        wr = sb("wr", [DIM, EXPERTS])
        br_row = sb("br_row", [1, EXPERTS])
        b1_t = sb("b1_t", [HID, EXPERTS])
        b2_b = sb("b2_b", [TOK, EXPERTS, DIM])
        lng_b = sb("lng_b", [TOK, DIM])
        lnb_b = sb("lnb_b", [TOK, DIM])
        bo_b = sb("bo_b", [TOK, DIM])
        bg_b = sb("bg_b", [TOK, INNER])
        gamma_b = sb("gamma_b", [TOK, DIM])
        beta_b = sb("beta_b", [TOK, DIM])
        ident = sb("ident", [128, 128])
        ident16 = sb("ident16", [128, 128], F16)
        ones = sb("ones", [128, 128])
        table_warm = sb("table_warm", [TOK, 1])
        neg_half = sb("neg_half", [TOK, ROWS])
        w_hi = sb("w_hi", [2 * DIM, 4 * INNER], F16)
        w_lo = sb("w_lo", [2 * DIM, 4 * INNER], F16)
        w1_split = sb("w1_split", [2 * DIM, 2, EXPERTS, HID], F16)
        stats = sb("stats", [TOK, ROWS, 6])
        stats2 = sb("stats2", [TOK, ROWS, 6])
        mv = sb("mv", [TOK, ROWS, 2])
        rstd = sb("rstd", [TOK, ROWS])
        xn = sb("xn", [TOK, ROWS, DIM])
        x_bo = sb("x_bo", [TOK, ROWS, DIM])
        x_split = sb("x_split", [TOK, ROWS, 2, DIM], F16)
        x_t = sb("x_t", [2 * DIM, ROWS, TOK], F16)
        qkg = sb("qkg", [TOK, 4, 3 * INNER])
        stack = sb("stack", [TOK, 4, 2 * (K_AT + 2 * SLOT)], F16)
        qk_t = sb("qk_t", [128, 2, 2, 4, TOK], F16)
        q2_t = sb("q2_t", [128, 2, 4, TOK], F16)
        v_aug = sb("v_aug", [TOK, 4, HEADS, VCOLS])
        gate = sb("gate", [TOK, 4, INNER])
        th = sb("th", [TOK, 4, INNER])
        prob = sb("prob", [TOK, 2, 2, 4, TOK])
        u_sb = sb("u_sb", [128, 2, 2, TOK])
        rden = sb("rden", [TOK, 4, HEADS])
        og1 = sb("og1", [TOK, 4, INNER])
        og = sb("og", [TOK, 4, INNER])
        og_t = sb("og_t", [INNER, 2, TOK])
        t_all = sb("t_all", [TOK, ROWS, DIM])
        mv2 = sb("mv2", [TOK, ROWS, 2])
        rstd2 = sb("rstd2", [TOK, ROWS])
        tn = sb("tn", [TOK, ROWS, DIM])
        tn_split = sb("tn_split", [TOK, ROWS, 2, DIM], F16)
        tn_t = sb("tn_t", [2 * DIM, ROWS, TOK], F16)
        tc = sb("tc", [TOK, ROWS, DIM])
        t_beta = sb("t_beta", [TOK, ROWS, DIM])
        mean_col = sb("mean_col", [DIM, 1])
        soft = sb("soft", [1, 3, EXPERTS])
        soft_max = sb("soft_max", [1, 3])
        soft_sum = sb("soft_sum", [1, 3])
        soft_inv = sb("soft_inv", [1, 3])
        capped = sb("capped", [1, EXPERTS])
        weights = sb("weights", [1, EXPERTS])
        top_v = sb("top_v", [1, EXPERTS])
        top_i = sb("top_i", [1, EXPERTS], U32)
        shares = sb("shares", [1, 2])
        shares_b = sb("shares_b", [128, 2])
        b2_pick = sb("b2_pick", [TOK, 2, DIM])
        b2_part = sb("b2_part", [TOK, 2, DIM])
        b2_sel = sb("b2_sel", [TOK, DIM])
        w1_sel = sb("w1_sel", [2 * DIM, 2, 2, HID], F16)
        w2_sel = sb("w2_sel", [HID, 2, DIM])
        b1_sel = sb("b1_sel", [HID, 2])
        hid = sb("hid", [HID, 2, TOKENS])
        tn_b2 = sb("tn_b2", [TOK, ROWS, DIM])
        z = sb("z", [TOK, ROWS, DIM])
        stats3 = sb("stats3", [TOK, ROWS, 6])
        mv3 = sb("mv3", [TOK, ROWS, 2])
        rstd3 = sb("rstd3", [TOK, ROWS])
        zc = sb("zc", [TOK, ROWS, DIM])
        zn = sb("zn", [TOK, ROWS, DIM])
        zg = sb("zg", [TOK, ROWS, DIM])
        res = sb("res", [TOK, ROWS, DIM])

        bank = [ctx.enter_context(nc.psum_tensor(f"bank{i}", [128, 512], F32)) for i in range(8)]
        B_PROJ, B_TQK, B_S1, B_S2, B_U, B_UT = 0, 1, 2, 4, 6, 7
        proj_p = bank[B_PROJ][:, :]
        ogt_p = bank[B_PROJ][:, 0:TOK]
        tqk_p = bank[B_TQK][:, :].bitcast(F16).rearrange("c (a p t) -> c a p t", a=2, p=4)
        tq2_p = bank[B_UT][:, 256:512].bitcast(F16).rearrange("c (p t) -> c p t", p=4)
        s1_p = [bank[B_S1 + a][:, :].rearrange("q (p k) -> q p k", p=4) for a in range(2)]
        s2_p = [bank[B_S2 + a][:, :].rearrange("k (p q) -> k p q", p=4) for a in range(2)]
        u_p = bank[B_U][:, 0:2 * TOK].rearrange("c (a q) -> c a q", a=2)
        ut_p = bank[B_UT][:, 0:2 * TOK].rearrange("q (h c) -> q h c", h=HEADS)
        y_p = bank[B_U][:, 2 * TOK:2 * TOK + DIM]
        x_tp_p = bank[B_U][:, 0:256].bitcast(F16).rearrange("c (s t) -> c s t", s=CHUNK)
        tn_tp_p = [bank[B_S1 + c][:, 0:256].bitcast(F16).rearrange("c (s t) -> c s t", s=CHUNK)
                   for c in range(CHUNKS)]
        mean_p = bank[B_TQK][0:DIM, 0:1]
        logits_p = bank[B_PROJ][0:1, 0:EXPERTS]
        shares_p = bank[7][:, 0:2]
        z_p = [bank[c][:, 0:CHUNK * DIM].rearrange("t (s d) -> t s d", s=CHUNK) for c in range(CHUNKS)]

        ld = {n: sem(f"loaded_{n}") for n in ("x0", "x1", "x2", "x3", "w", "lng", "lnb", "bo", "bg", "wo",
                                              "w1", "w2", "b1", "b2", "wr", "br", "gamma", "beta")}
        pool_order = sem("pool_order")
        dve_order = sem("dve_order")
        consts = sem("consts")
        ident_ok = sem("ident_ok")
        buffers_ok = sem("buffers_ok")
        w_hi_ok, w_lo_ok = sem("w_hi_ok"), sem("w_lo_ok")
        w1_hi_ok, w1_split_ok = sem("w1_hi_ok"), sem("w1_split_ok")
        mv_ok, rstd_ok, scaled_ok, xn_ok = sem("mv_ok"), sem("rstd_ok"), sem("scaled_ok"), sem("xn_ok")
        x_hi_ok, x_split_ok, x_tp, x_t_ok = sem("x_hi_ok"), sem("x_split_ok"), sem("x_tp"), sem("x_t_ok")
        x_bo_ok = sem("x_bo_ok")
        stats2_ok, mv2_ok, rstd2_ok, tn_ok = sem("stats2_ok"), sem("mv2_ok"), sem("rstd2_ok"), sem("tn_ok")
        tc_ok = sem("tc_ok")
        tn_hi_ok, tn_split_ok, tn_tp, tn_t_ok = sem("tn_hi_ok"), sem("tn_split_ok"), sem("tn_tp"), sem("tn_t_ok")
        proj_done, qkg_ok, proj_copied = sem("proj_done"), sem("qkg_ok"), sem("proj_copied")
        split_ok, gate_ok, tanh_done = sem("split_ok"), sem("gate_ok"), sem("tanh_done")
        tqk_done, tqk_copied = sem("tqk_done"), sem("tqk_copied")
        s1_done = [sem("s1_even_done"), sem("s1_odd_done")]
        max_done = [sem("max_even_done"), sem("max_odd_done")]
        tq2_done, tq2_copied = sem("tq2_done"), sem("tq2_copied")
        s2_done = [sem("s2_even_done"), sem("s2_odd_done")]
        exp_done = [sem("exp_even_done"), sem("exp_odd_done")]
        pv_done, u_copied, ut_done, ut_read = sem("pv_done"), sem("u_copied"), sem("ut_done"), sem("ut_read")
        og_ok, ogt_done, ogt_copied = sem("og_ok"), sem("ogt_done"), sem("ogt_copied")
        wo_done, t_ok = sem("wo_done"), sem("t_ok")
        mean_done, mean_ok, logits_done = sem("mean_done"), sem("mean_ok"), sem("logits_done")
        r_max, r_exp, top_i_ok = sem("r_max"), sem("r_exp"), sem("top_i_ok")
        shares_ok, shares_done, shares_b_ok = sem("shares_ok"), sem("shares_done"), sem("shares_b_ok")
        w1_sel_ok, b1_sel_ok, w2_sel_ok = sem("w1_sel_ok"), sem("b1_sel_ok"), sem("w2_sel_ok")
        fc1_done, gelu_done, fc2_done = sem("fc1_done"), sem("gelu_done"), sem("fc2_done")
        tn_b2_ok, t_beta_ok = sem("tn_b2_ok"), sem("t_beta_ok")
        z_ok, mv3_ok, rstd3_ok, zg_ok, zn_ok = sem("z_ok"), sem("mv3_ok"), sem("rstd3_ok"), sem("zg_ok"), sem("zn_ok")
        zg_pool_ok = sem("zg_pool_ok")
        stats3_ok, zc_ok = sem("stats3_ok"), sem("zc_ok")
        res_ok = [sem(f"res{c}_ok") for c in range(CHUNKS)]
        stored = sem("stored")

        block = ctx.enter_context(nc.Block())

        WIDE = [TOK, CHUNK, DIM]

        def live(s):
            return 0 <= s < ROWS

        def stack_slots(b, q_slot, k_slot):
            first = q_slot * SLOT
            apart = K_AT + (k_slot - q_slot) * SLOT
            v = stack[:, b, first:first + 2 * apart].rearrange("t (a c) -> t a c", a=2)
            return v[:, :, 0:QK].rearrange("t a (h c) -> t a h c", c=STACK)[:, :, :, 0:SLOT]

        def pair(b, which, p):
            first = which * K_AT + 2 * STACK * p
            return stack[:, b, first:first + 2 * STACK]

        @block.sync
        def _(sp):
            def twice(w):
                return w.unsqueeze(0).broadcast_to([2] + list(w.shape))

            def load_x(c):
                r = slice(c * CHUNK, (c + 1) * CHUNK)
                sp.dma_start(x_all[:, r, :], x_d[:, r, :]).then_inc(ld[f"x{c}"], 16)

            load_x(0)
            for dst, src in ((w_in[:, 0:INNER], Wq), (w_in[:, INNER:2 * INNER], Wkv[:, 0:INNER]),
                             (w_in[:, 2 * INNER:3 * INNER], Wg), (w_in[:, 3 * INNER:4 * INNER], Wkv[:, INNER:2 * INNER])):
                sp.dma_start(dst, twice(src)).then_inc(ld["w"], 16)
            load_x(1)
            load_x(2)
            load_x(3)
            sp.dma_start(wo[:, :], Wo).then_inc(ld["wo"], 16)
            for half in range(2):
                rows = slice(half * DIM, (half + 1) * DIM)
                sp.dma_start(w1_in[rows, :, :], W1.rearrange("e d f -> d e f")).then_inc(ld["w1"], 16)
            sp.dma_start(wr[:, :], Wr).then_inc(ld["wr"], 16)
            sp.dma_start(br_row[0:1, :], br.rearrange("(a e) -> a e", a=1)).then_inc(ld["br"], 16)
            sp.dma_start(w2_in[:, :, :], W2.rearrange("e f d -> f e d")).then_inc(ld["w2"], 16)
            sp.dma_start(b1_t[:, :], b1).then_inc(ld["b1"], 16)
            sp.dma_start(b2_b[:, :, :], b2.unsqueeze(0).broadcast_to([TOK, EXPERTS, DIM])).then_inc(ld["b2"], 16)
            for c in range(CHUNKS - 1):
                r = slice(c * CHUNK, (c + 1) * CHUNK)
                sp.wait_ge(res_ok[c], 1)
                sp.dma_start(out_d[:, r, :], res[:, r, :]).then_inc(stored, 16)
            sp.wait_ge(stored, 16 * CHUNKS)

        @block.scalar
        def _(act):
            act.wait_ge(consts, 2)
            nc.scalar.activation(table_warm[:, :], neg_half[:, 0:1], ACT.Exp)

            def bcast(v):
                return v.rearrange("(a d) -> a d", a=1).broadcast_to([TOK, v.shape[0]])

            for name, dst, src in (("lng", lng_b, ln_g), ("lnb", lnb_b, ln_b), ("bg", bg_b, bg), ("bo", bo_b, bo),
                                   ("gamma", gamma_b, gamma), ("beta", beta_b, beta)):
                act.dma_start(dst[:, :], bcast(src)).then_inc(ld[name], 16)

            def high_x(c):
                r = slice(c * CHUNK, (c + 1) * CHUNK)
                act.wait_ge(xn_ok, c + 1)
                nc.scalar.activation(x_split[:, r, 0, :], xn[:, r, :], ACT.Copy).then_inc(x_hi_ok, 1)

            def copy_x_t(c):
                act.wait_ge(x_tp, c + 1)
                nc.scalar.activation(x_t[:, c * CHUNK:(c + 1) * CHUNK, :], x_tp_p, ACT.Copy).then_inc(x_t_ok, 1)

            def projections(s):
                b = s % 4
                act.wait_ge(proj_done, s + 1)
                if s >= 4:
                    act.wait_ge(split_ok, s - 3)
                    act.wait_ge(gate_ok, s - 3)
                    act.wait_ge(tq2_done, s - 3)
                qk = proj_p[:, 0:2 * INNER].rearrange("t (a h c) -> t a h c", a=2, h=HEADS)
                nc.scalar.activation(stack_slots(b, 0, 0), qk, ACT.Copy, scale=1 / WSCALE)
                nc.scalar.activation(qkg[:, b, :], proj_p[:, 0:3 * INNER], ACT.Copy,
                                     scale=1 / WSCALE).then_inc(qkg_ok, 1)
                nc.scalar.activation(stack_slots(b, 1, 2), qk, ACT.Copy, scale=1 / WSCALE)
                if s >= 4:
                    act.wait_ge(pv_done, s - 3)
                nc.scalar.activation(v_aug[:, b, :, 0:HD],
                                     proj_p[:, 3 * INNER:4 * INNER].rearrange("t (h c) -> t h c", h=HEADS),
                                     ACT.Copy, scale=1 / WSCALE).then_inc(proj_copied, 1)

            def gates(s):
                b = s % 4
                act.wait_ge(gate_ok, s + 1)
                if s >= 4:
                    act.wait_ge(ut_read, s - 3)
                nc.scalar.activation(th[:, b, :], gate[:, b, :], ACT.Tanh, scale=0.5).then_inc(tanh_done, 1)

            def probabilities(s, a):
                act.wait_ge(s2_done[a], s + 1)
                if s >= 2:
                    act.wait_ge(pv_done, s - 1)
                nc.scalar.activation(prob[:, s % 2, a], s2_p[a], ACT.Exp, scale=HD ** -0.5).then_inc(exp_done[a], 1)

            def outputs(s):
                b = s % 2
                act.wait_ge(pv_done, s + 1)
                if s >= 2:
                    act.wait_ge(ut_done, s - 1)
                nc.scalar.activation(u_sb[:, b], u_p, ACT.Copy).then_inc(u_copied, 1)

            def gated(s):
                b = s % 2
                act.wait_ge(ogt_done, s + 1)
                if s >= 2:
                    act.wait_ge(wo_done, s - 1)
                nc.scalar.activation(og_t[:, b, :], ogt_p, ACT.Copy).then_inc(ogt_copied, 1)

            def high_w1(e):
                act.wait_ge(ld["w1"], 32)
                nc.scalar.activation(w1_split[:, 0, e:e + 2], w1_in[:, e:e + 2, :], ACT.Copy, scale=WSCALE).then_inc(w1_hi_ok, 1)

            def high_t(c):
                r = slice(c * CHUNK, (c + 1) * CHUNK)
                act.wait_ge(tn_ok, c + 1)
                nc.scalar.activation(tn_split[:, r, 0, :], tn[:, r, :], ACT.Copy).then_inc(tn_hi_ok, 1)

            def copy_tn_t(c):
                act.wait_ge(tn_tp, c + 1)
                nc.scalar.activation(tn_t[:, c * CHUNK:(c + 1) * CHUNK, :], tn_tp_p[c], ACT.Copy).then_inc(tn_t_ok, 1)

            high_x(0)
            act.wait_ge(ld["w"], 4 * 16)
            nc.scalar.activation(w_hi[:, :], w_in[:, :], ACT.Copy, scale=WSCALE).then_inc(w_hi_ok, 1)
            copy_x_t(0)
            for t in range(STEPS):
                for c in range(1, CHUNKS):
                    if t == SPLIT_AT[c]:
                        high_x(c)
                for c in range(1, CHUNKS):
                    if t == TRANSPOSE_AT[c]:
                        copy_x_t(c)
                if 0 <= t - W1_HIGH_AT < EXPERTS // 2:
                    high_w1(2 * (t - W1_HIGH_AT))
                if t == 14:
                    high_t(0)
                if t == 18:
                    high_t(1)
                if live(t):
                    projections(t)
                if live(t - 3):
                    outputs(t - 3)
                if live(t - 4):
                    gated(t - 4)
                if live(t - 2):
                    probabilities(t - 2, 0)
                if live(t - 1):
                    gates(t - 1)
                if live(t - 2):
                    probabilities(t - 2, 1)
            copy_tn_t(0)
            copy_tn_t(1)
            high_t(2)

            def exponentials(n, src, width):
                act.wait_ge(r_max, n + 1)
                nc.scalar.activation(soft[0:1, n, 0:width], src, ACT.Exp, bias=soft_max[0:1, n:n + 1],
                                     accum_out=soft_sum[0:1, n:n + 1]).then_inc(r_exp, 1)

            high_t(3)
            exponentials(0, logits_p, EXPERTS)
            copy_tn_t(2)
            exponentials(1, capped[0:1, :], EXPERTS)
            copy_tn_t(3)
            exponentials(2, top_v[0:1, 0:2], 2)
            nc.scalar.activation(table_warm[:, :], neg_half[:, 0:1], ACT.Gelu)
            act.wait_ge(b1_sel_ok, 2)
            for c in range(CHUNKS):
                for j in range(2):
                    n = 2 * c + j
                    act.wait_ge(fc1_done, n + 1)
                    nc.scalar.activation(hid[:, j, c * 512:(c + 1) * 512], bank[n][:, :], ACT.Gelu,
                                         bias=b1_sel[:, j:j + 1], scale=1 / WSCALE).then_inc(gelu_done, 1)
            for c in range(CHUNKS - 1):
                if c < 2:
                    act.wait_ge(zg_pool_ok, c + 1)
                else:
                    act.wait_ge(zg_ok, 1)
                act.wait_ge(rstd3_ok, c + 1)
                for s in range(c * CHUNK, (c + 1) * CHUNK):
                    last = nc.scalar.activation(zn[:, s, :], zg[:, s, :], ACT.Copy, scale=rstd3[:, s:s + 1])
                last.then_inc(zn_ok, 1)
            r = slice((CHUNKS - 1) * CHUNK, ROWS)
            act.wait_ge(res_ok[CHUNKS - 1], 1)
            act.dma_start(out_d[:, r, :], res[:, r, :]).then_inc(stored, 16)

        @block.vector
        def _(dve):
            order = [0]

            def then_next(instruction):
                order[0] += 1
                instruction.then_inc(dve_order, 1)
                dve.wait_ge(dve_order, order[0])

            nc.vector.memset(ones[:, :], 1.0).then_inc(consts, 1)
            nc.vector.memset(neg_half[:, :], -0.5).then_inc(consts, 1)

            def moments(c, src, stats, mv_, mv_sem):
                rows = range(c * CHUNK, (c + 1) * CHUNK)
                for s in rows:
                    last = nc.vector.bn_stats(stats[:, s, :], src[:, s, :])
                then_next(last)
                for s in rows:
                    last = nc.vector.bn_aggr(mv_[:, s, :], stats[:, s, :])
                last.then_inc(mv_sem, 1)

            def centered(c, src, mv_, mv_sem, dst):
                r = slice(c * CHUNK, (c + 1) * CHUNK)
                dve.wait_ge(mv_sem, c + 1)
                then_next(nc.vector.tensor_tensor(dst[:, r, :], src[:, r, :], mv_[:, r, 0:1].broadcast_to(WIDE), ALU.subtract))

            def scaled(c, rstd_, rstd_sem, dst):
                r = slice(c * CHUNK, (c + 1) * CHUNK)
                dve.wait_ge(rstd_sem, c + 1)
                return nc.vector.tensor_tensor(dst[:, r, :], dst[:, r, :], rstd_[:, r].unsqueeze(2).broadcast_to(WIDE), ALU.mult)

            def norm_x(c):
                centered(c, x_all, mv, mv_ok, xn)
                scaled(c, rstd, rstd_ok, xn).then_inc(scaled_ok, 1)

            def weight_x(c):
                r = slice(c * CHUNK, (c + 1) * CHUNK)
                dve.wait_ge(scaled_ok, c + 1)
                dve.wait_ge(ld["lng"], 16)
                then_next(nc.vector.tensor_tensor(xn[:, r, :], xn[:, r, :], lng_b[:, :].unsqueeze(1).broadcast_to(WIDE), ALU.mult))
                dve.wait_ge(ld["lnb"], 16)
                nc.vector.tensor_tensor(xn[:, r, :], xn[:, r, :], lnb_b[:, :].unsqueeze(1).broadcast_to(WIDE),
                                        ALU.add).then_inc(xn_ok, 1)

            def low_x(c):
                r = slice(c * CHUNK, (c + 1) * CHUNK)
                dve.wait_ge(x_hi_ok, c + 1)
                nc.vector.tensor_tensor(x_split[:, r, 1, :], xn[:, r, :], x_split[:, r, 0, :], ALU.subtract).then_inc(x_split_ok, 1)

            def copy_stacks(s):
                b = s % 2
                dve.wait_ge(tqk_done, s + 1)
                if s >= 2:
                    for a in range(2):
                        dve.wait_ge(s2_done[a], s - 1)
                nc.vector.tensor_copy(qk_t[:, b], tqk_p).then_inc(tqk_copied, 1)

            def maxima(s):
                b = s % 4
                for a in range(2):
                    dve.wait_ge(s1_done[a], s + 1)
                    q = stack[:, b, 0:QK].rearrange("t (p a c) -> t p a c", p=4, a=2)
                    nc.vector.tensor_reduce(q[:, :, a, SHIFT], s1_p[a], AX, ALU.max, negate=True).then_inc(max_done[a], 1)

            def copy_q(s):
                b = s % 2
                dve.wait_ge(tq2_done, s + 1)
                if s >= 2:
                    for a in range(2):
                        dve.wait_ge(s2_done[a], s - 1)
                nc.vector.tensor_copy(q2_t[:, b], tq2_p).then_inc(tq2_copied, 1)

            def gate_outputs(s):
                b = s % 4
                dve.wait_ge(ut_done, s + 1)
                dve.wait_ge(tanh_done, s + 1)
                if s >= 4:
                    dve.wait_ge(og_ok, s - 3)
                nc.vector.reciprocal(rden[:, b, :], ut_p[:, :, HD])
                nc.vector.scalar_tensor_tensor(out=og1[:, b, :].rearrange("t (h c) -> t h c", h=HEADS),
                                               in0=th[:, b, :].rearrange("t (h c) -> t h c", h=HEADS), scalar=1.0,
                                               in1=ut_p[:, :, 0:HD], op0=ALU.add, op1=ALU.mult).then_inc(ut_read, 1)

            def residual(s):
                dve.wait_ge(wo_done, s + 1)
                dve.wait_ge(x_bo_ok, s // CHUNK + 1)
                nc.vector.tensor_tensor(t_all[:, s, :], y_p, x_bo[:, s, :], ALU.add).then_inc(t_ok, 1)

            def row_stats(s):
                dve.wait_ge(t_ok, s + 1)
                nc.vector.bn_stats(stats2[:, s, :], t_all[:, s, :]).then_inc(stats2_ok, 1)

            def row_moments(s):
                dve.wait_ge(stats2_ok, s + 1)
                nc.vector.bn_aggr(mv2[:, s, :], stats2[:, s, :]).then_inc(mv2_ok, 1)

            def norm_t(c):
                r = slice(c * CHUNK, (c + 1) * CHUNK)
                dve.wait_ge(mv2_ok, (c + 1) * CHUNK)
                nc.vector.tensor_tensor(tc[:, r, :], t_all[:, r, :], mv2[:, r, 0:1].broadcast_to(WIDE),
                                        ALU.subtract).then_inc(tc_ok, 1)
                dve.wait_ge(tc_ok, c + 1)
                dve.wait_ge(rstd2_ok, c + 1)
                nc.vector.tensor_tensor(tn[:, r, :], tc[:, r, :], rstd2[:, r].unsqueeze(2).broadcast_to(WIDE),
                                        ALU.mult).then_inc(tn_ok, 1)

            def low_w1(e):
                dve.wait_ge(w1_hi_ok, e // 2 + 1)
                nc.vector.scalar_tensor_tensor(out=w1_split[:, 1, e:e + 2], in0=w1_in[:, e:e + 2, :], scalar=WSCALE,
                                               in1=w1_split[:, 0, e:e + 2], op0=ALU.mult,
                                               op1=ALU.subtract).then_inc(w1_split_ok, 1)

            dve.wait_ge(ld["x0"], 16)
            moments(0, x_all, stats, mv, mv_ok)
            norm_x(0)
            weight_x(0)
            low_x(0)
            dve.wait_ge(w_hi_ok, 1)
            nc.vector.scalar_tensor_tensor(out=w_lo[:, :], in0=w_in[:, :], scalar=WSCALE, in1=w_hi[:, :],
                                           op0=ALU.mult, op1=ALU.subtract).then_inc(w_lo_ok, 1)
            for c in range(1, CHUNKS):
                dve.wait_ge(ld[f"x{c}"], 16)
                moments(c, x_all, stats, mv, mv_ok)
            norm_x(1)
            dve.wait_ge(buffers_ok, 1)

            for t in range(STEPS):
                for c in range(1, CHUNKS):
                    if t == SPLIT_AT[c]:
                        low_x(c)
                for c in range(2, CHUNKS):
                    if t == NORM_AT[c]:
                        norm_x(c)
                for c in range(1, CHUNKS):
                    if t == WEIGHT_AT[c]:
                        weight_x(c)
                if 0 <= t - W1_LOW_AT < EXPERTS // 2:
                    low_w1(2 * (t - W1_LOW_AT))
                if live(t - 1):
                    maxima(t - 1)
                if live(t - 3):
                    gate_outputs(t - 3)
                if live(t - 5):
                    residual(t - 5)
                if live(t - 6):
                    row_stats(t - 6)
                if live(t - 7):
                    row_moments(t - 7)
                if live(t):
                    copy_stacks(t)
                if live(t - 1):
                    copy_q(t - 1)
            norm_t(2)
            norm_t(3)

            dve.wait_ge(mean_done, 1)
            nc.vector.tensor_scalar(mean_col[:, :], mean_p, 1.0 / TOKENS, None, ALU.mult).then_inc(mean_ok, 1)
            dve.wait_ge(logits_done, 1)
            nc.vector.tensor_reduce(soft_max[0:1, 0:1], logits_p, AX, ALU.max, negate=True).then_inc(r_max, 1)
            dve.wait_ge(r_exp, 1)
            then_next(nc.vector.reciprocal(soft_inv[0:1, 0:1], soft_sum[0:1, 0:1]))
            then_next(nc.vector.tensor_scalar(capped[0:1, :], soft[0:1, 0, :], soft_inv[0:1, 0:1], CAPACITY / TOKENS,
                                              ALU.mult, ALU.min))
            nc.vector.tensor_reduce(soft_max[0:1, 1:2], capped[0:1, :], AX, ALU.max, negate=True).then_inc(r_max, 1)
            dve.wait_ge(r_exp, 2)
            then_next(nc.vector.reciprocal(soft_inv[0:1, 1:2], soft_sum[0:1, 1:2]))
            then_next(nc.vector.tensor_scalar(weights[0:1, :], soft[0:1, 1, :], soft_inv[0:1, 1:2], None, ALU.mult))
            then_next(nc.vector.max(top_v[0:1, :], weights[0:1, :]))
            nc.vector.tensor_scalar(soft_max[0:1, 2:3], top_v[0:1, 0:1], -1.0, None, ALU.mult).then_inc(r_max, 1)
            nc.vector.max_index(top_i[0:1, :], top_v[0:1, :], weights[0:1, :]).then_inc(top_i_ok, 1)
            dve.wait_ge(top_i_ok, 1)
            expert = [dve.value_load(top_i[0:1, j:j + 1], min_val=0, max_val=EXPERTS - 1) for j in range(2)]
            dve.wait_ge(w1_split_ok, EXPERTS // 2)
            for j in range(2):
                nc.vector.tensor_copy(w1_sel[:, j], w1_split[:, :, bass.ds(expert[j], 1), :].rearrange(
                    "c l e f -> c l (e f)")).then_inc(w1_sel_ok, 1)
            dve.wait_ge(r_exp, 3)
            then_next(nc.vector.reciprocal(soft_inv[0:1, 2:3], soft_sum[0:1, 2:3]))
            nc.vector.tensor_scalar(shares[0:1, :], soft[0:1, 2, 0:2], soft_inv[0:1, 2:3], None, ALU.mult).then_inc(shares_ok, 1)
            dve.wait_ge(shares_done, 1)
            nc.vector.tensor_copy(shares_b[:, :], shares_p).then_inc(shares_b_ok, 1)
            dve.wait_ge(shares_b_ok, 1)
            dve.wait_ge(ld["w2"], 16)
            for j in range(2):
                nc.vector.tensor_scalar(w2_sel[:, j, :], w2_in[:, bass.ds(expert[j], 1), :].rearrange("f e d -> f (e d)"),
                                        shares_b[:, j:j + 1], None, ALU.mult).then_inc(w2_sel_ok, 1)

            def add_z(c):
                r = slice(c * CHUNK, (c + 1) * CHUNK)
                dve.wait_ge(fc2_done, c + 1)
                dve.wait_ge(tn_b2_ok, c + 1)
                nc.vector.tensor_tensor(z[:, r, :], z_p[c], tn_b2[:, r, :], ALU.add).then_inc(z_ok, 1)

            def stats_z(c):
                dve.wait_ge(z_ok, c + 1)
                for s in range(c * CHUNK, (c + 1) * CHUNK):
                    last = nc.vector.bn_stats(stats3[:, s, :], z[:, s, :])
                last.then_inc(stats3_ok, 1)

            def moments_z(c):
                dve.wait_ge(stats3_ok, c + 1)
                for s in range(c * CHUNK, (c + 1) * CHUNK):
                    last = nc.vector.bn_aggr(mv3[:, s, :], stats3[:, s, :])
                last.then_inc(mv3_ok, 1)

            def center_z(c):
                r = slice(c * CHUNK, (c + 1) * CHUNK)
                dve.wait_ge(mv3_ok, c + 1)
                nc.vector.tensor_tensor(zc[:, r, :], z[:, r, :], mv3[:, r, 0:1].broadcast_to(WIDE), ALU.subtract).then_inc(zc_ok, 1)

            def weight_z(c):
                r = slice(c * CHUNK, (c + 1) * CHUNK)
                dve.wait_ge(zc_ok, c + 1)
                dve.wait_ge(ld["gamma"], 16)
                nc.vector.tensor_tensor(zg[:, r, :], zc[:, r, :], gamma_b[:, :].unsqueeze(1).broadcast_to(WIDE),
                                        ALU.mult).then_inc(zg_ok, 1)

            for c in range(CHUNKS):
                add_z(c)
                stats_z(c)
                if c == 3:
                    weight_z(2)
                moments_z(c)
                center_z(c)
            weight_z(CHUNKS - 1)
            c = CHUNKS - 2
            r = slice(c * CHUNK, (c + 1) * CHUNK)
            dve.wait_ge(t_beta_ok, CHUNKS)
            dve.wait_ge(zn_ok, CHUNKS - 1)
            nc.vector.tensor_tensor(res[:, r, :], zn[:, r, :], t_beta[:, r, :], ALU.add).then_inc(res_ok[c], 1)
            c = CHUNKS - 1
            dve.wait_ge(rstd3_ok, c + 1)
            dve.wait_ge(zg_ok, 2)
            for s in range(c * CHUNK, ROWS):
                last = nc.vector.scalar_tensor_tensor(out=res[:, s, :], in0=zg[:, s, :], scalar=rstd3[:, s:s + 1],
                                                      in1=t_beta[:, s, :], op0=ALU.mult, op1=ALU.add)
            last.then_inc(res_ok[c], 1)

        @block.gpsimd
        def _(pool):
            order = [0]

            def then_next(instruction):
                order[0] += 1
                instruction.then_inc(pool_order, 1)
                pool.wait_ge(pool_order, order[0])

            def power(c, mv_, rstd_, scale, eps, rstd_sem):
                r = slice(c * CHUNK, (c + 1) * CHUNK)
                then_next(nc.gpsimd.tensor_scalar(rstd_[:, r], mv_[:, r, 1], scale, eps, ALU.mult, ALU.add))
                nc.gpsimd.tensor_tensor(rstd_[:, r], rstd_[:, r], neg_half[:, r], ALU.pow).then_inc(rstd_sem, 1)

            def power_x(c):
                pool.wait_ge(mv_ok, c + 1)
                power(c, mv, rstd, 1.0 + EPS_LN, EPS_LN * EPS_OUTER, rstd_ok)

            def add_bo(c):
                r = slice(c * CHUNK, (c + 1) * CHUNK)
                pool.wait_ge(ld[f"x{c}"], 16)
                pool.wait_ge(ld["bo"], 16)
                nc.gpsimd.tensor_tensor(x_bo[:, r, :], x_all[:, r, :], bo_b[:, :].unsqueeze(1).broadcast_to(WIDE),
                                        ALU.add).then_inc(x_bo_ok, 1)

            def power_t(c):
                pool.wait_ge(mv2_ok, (c + 1) * CHUNK)
                power(c, mv2, rstd2, 1.0, EPS_LN, rstd2_ok)

            def center_t(c):
                r = slice(c * CHUNK, (c + 1) * CHUNK)
                pool.wait_ge(mv2_ok, (c + 1) * CHUNK)
                nc.gpsimd.tensor_tensor(tc[:, r, :], t_all[:, r, :], mv2[:, r, 0:1].broadcast_to(WIDE),
                                        ALU.subtract).then_inc(tc_ok, 1)

            def scale_t(c):
                r = slice(c * CHUNK, (c + 1) * CHUNK)
                pool.wait_ge(tc_ok, c + 1)
                pool.wait_ge(rstd2_ok, c + 1)
                nc.gpsimd.tensor_tensor(tn[:, r, :], tc[:, r, :], rstd2[:, r].unsqueeze(2).broadcast_to(WIDE),
                                        ALU.mult).then_inc(tn_ok, 1)

            def low_t(c):
                r = slice(c * CHUNK, (c + 1) * CHUNK)
                pool.wait_ge(tn_ok, c + 1)
                pool.wait_ge(tn_hi_ok, c + 1)
                nc.gpsimd.tensor_tensor(tn_split[:, r, 1, :], tn[:, r, :], tn_split[:, r, 0, :], ALU.subtract).then_inc(tn_split_ok, 1)

            def add_beta(c):
                r = slice(c * CHUNK, (c + 1) * CHUNK)
                pool.wait_ge(ld["beta"], 16)
                pool.wait_ge(t_ok, (c + 1) * CHUNK)
                nc.gpsimd.tensor_tensor(t_beta[:, r, :], t_all[:, r, :], beta_b[:, :].unsqueeze(1).broadcast_to(WIDE),
                                        ALU.add).then_inc(t_beta_ok, 1)

            def gate_input(s):
                b = s % 4
                pool.wait_ge(qkg_ok, s + 1)
                if s >= 4:
                    pool.wait_ge(tanh_done, s - 3)
                nc.gpsimd.tensor_tensor(gate[:, b, :], qkg[:, b, 2 * INNER:3 * INNER], bg_b[:, :], ALU.add).then_inc(gate_ok, 1)

            def low(s):
                b = s % 4
                pool.wait_ge(qkg_ok, s + 1)
                nc.gpsimd.tensor_tensor(stack_slots(b, 2, 1),
                                        qkg[:, b, 0:2 * INNER].rearrange("t (a h c) -> t a h c", a=2, h=HEADS),
                                        stack_slots(b, 0, 0), ALU.subtract).then_inc(split_ok, 1)

            def divide(s):
                b = s % 4
                pool.wait_ge(ut_read, s + 1)
                if s >= 4:
                    pool.wait_ge(ogt_done, s - 3)
                nc.gpsimd.tensor_tensor(og[:, b, :].rearrange("t (h c) -> t h c", h=HEADS),
                                        og1[:, b, :].rearrange("t (h c) -> t h c", h=HEADS),
                                        rden[:, b, :].unsqueeze(2).broadcast_to([TOK, HEADS, HD]),
                                        ALU.mult).then_inc(og_ok, 1)

            pool.wait_ge(consts, 2)
            nc.gpsimd.affine_select(out=ident[:, :], in_=ones[:, :], compare_op=ALU.is_equal, fill=0.0, base=0,
                                    pattern=[[-1, 128]], channel_multiplier=1).then_inc(ident_ok, 1)
            pool.wait_ge(ident_ok, 1)
            nc.gpsimd.tensor_copy(ident16[:, :], ident[:, :]).then_inc(ident_ok, 1)
            power_x(0)
            for first in (0, K_AT):
                v = stack[:, :, first:first + QK].rearrange("t b (h c) -> t b h c", c=STACK)
                nc.gpsimd.memset(v[:, :, :, SHIFT:STACK], 0.0)
            then_next(nc.gpsimd.memset(v_aug[:, :, :, HD:VCOLS], 0.0))
            nc.gpsimd.memset(v[:, :, :, SHIFT], 1.0)
            then_next(nc.gpsimd.memset(v_aug[:, :, :, HD], 2.0))
            pool.sem_inc(buffers_ok, 1)
            power_x(1)
            pool.wait_ge(ld["bg"], 16)
            for t in range(STEPS):
                if t in (1, 2):
                    power_x(t + 1)
                if t in (3, 6, 8, 10):
                    add_bo((3, 6, 8, 10).index(t))
                for c in range(2):
                    if t == 11 + 4 * c:
                        center_t(c)
                    if t == 12 + 4 * c:
                        power_t(c)
                    if t == 13 + 4 * c:
                        scale_t(c)
                    if t == 14 + 4 * c:
                        low_t(c)
                if live(t):
                    low(t)
                    gate_input(t)
                if live(t - 3):
                    divide(t - 3)
            power_t(2)
            power_t(3)
            low_t(2)
            low_t(3)
            for c in range(CHUNKS):
                add_beta(c)
            pool.wait_ge(top_i_ok, 1)
            expert = [pool.value_load(top_i[0:1, j:j + 1], min_val=0, max_val=EXPERTS - 1) for j in range(2)]
            pool.wait_ge(ld["b1"], 16)
            for j in range(2):
                nc.gpsimd.tensor_copy(b1_sel[:, j:j + 1], b1_t[:, bass.ds(expert[j], 1)]).then_inc(b1_sel_ok, 1)
            pool.wait_ge(ld["b2"], 16)
            for j in range(2):
                last = nc.gpsimd.tensor_copy(b2_pick[:, j, :], b2_b[:, bass.ds(expert[j], 1), :].rearrange("t e d -> t (e d)"))
            then_next(last)
            pool.wait_ge(shares_b_ok, 1)
            for j in range(2):
                last = nc.gpsimd.tensor_scalar(b2_part[:, j, :], b2_pick[:, j, :], shares_b[:, j:j + 1], None, ALU.mult)
            then_next(last)
            then_next(nc.gpsimd.tensor_tensor(b2_sel[:, :], b2_part[:, 0, :], b2_part[:, 1, :], ALU.add))
            for c in range(CHUNKS):
                r = slice(c * CHUNK, (c + 1) * CHUNK)
                nc.gpsimd.tensor_tensor(tn_b2[:, r, :], tn[:, r, :], b2_sel[:, :].unsqueeze(1).broadcast_to(WIDE),
                                        ALU.add).then_inc(tn_b2_ok, 1)
            for c in range(CHUNKS):
                pool.wait_ge(mv3_ok, c + 1)
                power(c, mv3, rstd3, 1.0, EPS_LN, rstd3_ok)
                if c < 2:
                    r = slice(c * CHUNK, (c + 1) * CHUNK)
                    pool.wait_ge(zc_ok, c + 1)
                    pool.wait_ge(ld["gamma"], 16)
                    nc.gpsimd.tensor_tensor(zg[:, r, :], zc[:, r, :], gamma_b[:, :].unsqueeze(1).broadcast_to(WIDE),
                                            ALU.mult).then_inc(zg_pool_ok, 1)
                if 0 < c < CHUNKS - 1:
                    r = slice((c - 1) * CHUNK, c * CHUNK)
                    pool.wait_ge(zn_ok, c)
                    nc.gpsimd.tensor_tensor(res[:, r, :], zn[:, r, :], t_beta[:, r, :], ALU.add).then_inc(res_ok[c - 1], 1)

        @block.tensor
        def _(pe):
            def transpose_x(c):
                pe.wait_ge(x_split_ok, c + 1)
                if c > 0:
                    pe.wait_ge(x_t_ok, c)
                if TRANSPOSE_AT[c] > 3:
                    pe.wait_ge(u_copied, TRANSPOSE_AT[c] - 3)
                if TRANSPOSE_AT[c] > 5:
                    pe.wait_ge(t_ok, TRANSPOSE_AT[c] - 5)
                for i in range(CHUNK):
                    last = nc.tensor.transpose(x_tp_p[:, i, :], x_split[:, c * CHUNK + i].rearrange("t l d -> t (l d)"),
                                               ident16[:, :])
                last.then_inc(x_tp, 1)

            def project(s):
                pe.wait_ge(x_t_ok, s // CHUNK + 1)
                if s > 0:
                    pe.wait_ge(proj_copied, s)
                if s > GATED_LATE:
                    pe.wait_ge(ogt_copied, s - GATED_LATE)
                nc.tensor.matmul(proj_p, x_t[:, s, :], w_hi[:, :], start=True, stop=False)
                nc.tensor.matmul(proj_p, x_t[:, s, :], w_lo[:, :], start=False, stop=True).then_inc(proj_done, 1)

            def transpose_stacks(s):
                b = s % 4
                pe.wait_ge(split_ok, s + 1)
                pe.wait_ge(proj_copied, s + 1)
                if s > 0:
                    pe.wait_ge(tqk_copied, s)
                for which in range(2):
                    for p in range(4):
                        last = nc.tensor.transpose(tqk_p[:, which, p, :], pair(b, which, p), ident16[:, :])
                last.then_inc(tqk_done, 1)

            def scores(s, a):
                b, r = s % 2, slice(64 * a, 64 * a + SHIFT)
                pe.wait_ge(tqk_copied, s + 1)
                if s > 0:
                    pe.wait_ge(max_done[a], s)
                for p in range(4):
                    last = nc.tensor.matmul(s1_p[a][:, p, :], qk_t[r, b, 0, p, :], qk_t[r, b, 1, p, :],
                                            start=True, stop=True)
                last.then_inc(s1_done[a], 1)

            def transpose_q(s):
                b = s % 4
                for a in range(2):
                    pe.wait_ge(max_done[a], s + 1)
                if s > 0:
                    pe.wait_ge(tq2_copied, s)
                if s > 1:
                    pe.wait_ge(ut_read, s - 1)
                for p in range(4):
                    last = nc.tensor.transpose(tq2_p[:, p, :], pair(b, 0, p), ident16[:, :])
                last.then_inc(tq2_done, 1)

            def shifted_scores(s, a):
                b, r = s % 2, slice(64 * a, 64 * a + STACK)
                pe.wait_ge(tq2_copied, s + 1)
                if s > 0:
                    pe.wait_ge(exp_done[a], s)
                for p in range(4):
                    last = nc.tensor.matmul(s2_p[a][:, p, :], qk_t[r, b, 1, p, :], q2_t[r, b, p, :],
                                            start=True, stop=True)
                last.then_inc(s2_done[a], 1)

            def values(s):
                b = s % 4
                for a in range(2):
                    pe.wait_ge(exp_done[a], s + 1)
                pe.wait_ge(proj_copied, s + 1)
                pe.wait_ge(x_t_ok, sum(at <= s + 3 for at in TRANSPOSE_AT))
                if s > 0:
                    pe.wait_ge(u_copied, s)
                if s > 2:
                    pe.wait_ge(t_ok, s - 2)
                for a in range(2):
                    for p in range(4):
                        last = nc.tensor.matmul(u_p[32 * p:32 * p + 32, a, :], v_aug[:, b, 2 * p + a, :],
                                                prob[:, s % 2, a, p, :], start=True, stop=True)
                last.then_inc(pv_done, 1)

            def transpose_outputs(s):
                pe.wait_ge(u_copied, s + 1)
                pe.wait_ge(tq2_copied, min(s + 2, ROWS))
                if s == ROWS - 1:
                    pe.wait_ge(ut_read, s)
                for a in range(2):
                    last = nc.tensor.transpose(ut_p.rearrange("q (p a) c -> q p a c", a=2)[:, :, a, :],
                                               u_sb[:, s % 2, a, :], ident[:, :])
                last.then_inc(ut_done, 1)

            def transpose_gated(s):
                pe.wait_ge(og_ok, s + 1)
                pe.wait_ge(proj_copied, min(s + GATED_LATE + 1, ROWS))
                if s > 0:
                    pe.wait_ge(ogt_copied, s)
                nc.tensor.transpose(ogt_p, og[:, s % 4, :], ident[:, :]).then_inc(ogt_done, 1)

            def project_out(s):
                if s == 0:
                    pe.wait_ge(ld["wo"], 16)
                pe.wait_ge(ogt_copied, s + 1)
                pe.wait_ge(u_copied, min(s + 3, ROWS))
                if s > 0:
                    pe.wait_ge(t_ok, s)
                nc.tensor.matmul(y_p, og_t[:, s % 2, :], wo[:, :], start=True, stop=True).then_inc(wo_done, 1)

            def sum_tokens(c):
                pe.wait_ge(tc_ok, c + 1)
                pe.wait_ge(rstd2_ok, c + 1)
                if c == 0:
                    pe.wait_ge(tqk_copied, ROWS)
                for s in range(c * CHUNK, (c + 1) * CHUNK):
                    last = nc.tensor.matmul(mean_p, tc[:, s, :], rstd2[:, s:s + 1], start=s == 0, stop=s == ROWS - 1)
                if c == CHUNKS - 1:
                    last.then_inc(mean_done, 1)

            def transpose_tn(c):
                pe.wait_ge(tn_split_ok, c + 1)
                if c < 2:
                    pe.wait_ge(max_done[c], ROWS)
                else:
                    pe.wait_ge(exp_done[c - 2], ROWS)
                for i in range(CHUNK):
                    last = nc.tensor.transpose(tn_tp_p[c][:, i, :],
                                               tn_split[:, c * CHUNK + i].rearrange("t l d -> t (l d)"), ident16[:, :])
                last.then_inc(tn_tp, 1)

            def stay_warm(target, columns, count):
                with pe.Fori(0, count):
                    for _ in range(4):
                        nc.tensor.matmul(target, ident16[:, :], columns, start=True, stop=True)

            pe.wait_ge(ident_ok, 2)
            stay_warm(bank[B_S1][:, 0:256], ones[:, :].bitcast(F16), WARM_START)
            transpose_x(0)
            pe.wait_ge(w_hi_ok, 1)
            pe.wait_ge(w_lo_ok, 1)

            def between_last_rows():
                pe.wait_ge(tqk_copied, ROWS)
                stay_warm(bank[B_TQK][:, 0:256], ones[:, :].bitcast(F16), 1)

            for t in range(STEPS):
                if t == 1:
                    pe.wait_ge(buffers_ok, 1)
                for c in range(1, CHUNKS):
                    if t == TRANSPOSE_AT[c]:
                        transpose_x(c)
                for _ in range({18: 1, 19: 2, 20: 1}.get(t, 0)):
                    between_last_rows()
                if t == 19:
                    transpose_tn(0)
                    transpose_tn(1)
                if live(t):
                    project(t)
                if live(t - 1):
                    transpose_stacks(t - 1)
                if live(t - 2):
                    transpose_q(t - 2)
                if live(t - 3):
                    values(t - 3)
                if live(t - 1):
                    scores(t - 1, 0)
                if live(t - GATED_LATE):
                    transpose_gated(t - GATED_LATE)
                if live(t - 1):
                    scores(t - 1, 1)
                if live(t - 2):
                    shifted_scores(t - 2, 0)
                    shifted_scores(t - 2, 1)
                if live(t - 3):
                    transpose_outputs(t - 3)
                if live(t - 5):
                    project_out(t - 5)
            pe.wait_ge(ld["wr"], 16)
            pe.wait_ge(ld["br"], 16)
            nc.tensor.matmul(logits_p, ones[0:1, 0:1], br_row[0:1, :], start=True, stop=False)
            for c in range(CHUNKS):
                sum_tokens(c)
                if c == CHUNKS - 2:
                    pe.wait_ge(t_ok, ROWS)
                    stay_warm(bank[B_U][:, 0:256], ones[:, :].bitcast(F16), WARM_NORM)
            pe.wait_ge(mean_ok, 1)
            nc.tensor.matmul(logits_p, mean_col[:, :], wr[:, :], start=False, stop=True).then_inc(logits_done, 1)
            transpose_tn(2)
            transpose_tn(3)
            stay_warm(bank[B_U][:, 0:256], ones[:, :].bitcast(F16), WARM_ROUTING)

            def fc1(c):
                pe.wait_ge(tn_t_ok, c + 1)
                for j in range(2):
                    n = 2 * c + j
                    if c == 0:
                        pe.wait_ge(w1_sel_ok, j + 1)
                    if n in (2, 4):
                        pe.wait_ge(tn_t_ok, n // 2 + 2)
                    if n == 7:
                        pe.wait_ge(shares_b_ok, 1)
                    for part in range(2):
                        last = nc.tensor.matmul(bank[n][:, :], w1_sel[:, j, part, :],
                                                tn_t[:, c * CHUNK:(c + 1) * CHUNK, :].rearrange("c s t -> c (s t)"),
                                                start=part == 0, stop=part == 1)
                    last.then_inc(fc1_done, 1)

            def fc2(c):
                pe.wait_ge(gelu_done, 2 * c + 2)
                pe.wait_ge(w2_sel_ok, 2)
                for i in range(CHUNK):
                    s = c * CHUNK + i
                    for j in range(2):
                        last = nc.tensor.matmul(z_p[c][:, i, :], hid[:, j, s * TOK:(s + 1) * TOK], w2_sel[:, j, :],
                                                start=j == 0, stop=j == 1)
                last.then_inc(fc2_done, 1)

            fc1(0)
            pe.wait_ge(shares_ok, 1)
            nc.tensor.matmul(shares_p, ones[0:1, :], shares[0:1, :], start=True, stop=True).then_inc(shares_done, 1)
            fc1(1)
            for c in range(CHUNKS):
                fc2(c)
                if c + 2 < CHUNKS:
                    fc1(c + 2)


_ORDER = ["x", "L0_conv_ln_g", "L0_conv_ln_b", "L0_conv_Wq", "L0_conv_Wkv", "L0_conv_Wg", "L0_conv_bg", "L0_conv_Wo",
          "L0_conv_bo", "L0_ffn_Wr", "L0_ffn_br", "L0_ffn_W1", "L0_ffn_b1", "L0_ffn_W2", "L0_ffn_b2", "L0_ffn_gamma",
          "L0_ffn_beta"]

_COLUMNS = ("L0_ffn_b1",)


def kernel(**inputs):
    import numpy as _np
    import concourse.bacc as _bacc
    from concourse import mybir as _mybir
    from concourse.bass_utils import run_bass_kernel_spmd as _run

    nc = _bacc.Bacc("TRN2", target_bir_lowering=False, num_devices=1)
    arrays, args = {}, []
    for name in _ORDER:
        a = _np.asarray(inputs[name])
        if name in _COLUMNS:
            a = a.T
        a = _np.ascontiguousarray(a)
        arrays[f"in_{name}"] = a
        args.append(nc.dram_tensor(f"in_{name}", a.shape, _mybir.dt.from_np(a.dtype), kind="ExternalInput").ap())
    args.append(nc.dram_tensor("out_0", (1, ROWS, TOK, DIM), _mybir.dt.float32, kind="ExternalOutput").ap())
    metaformer_kernel(nc, *args)
    return _run(nc, [arrays], core_ids=[0]).results[0]["out_0"]
```
